# Optimizing a Trainium2 kernel written in Bass

```python
import numpy as np
import jax
import jax.numpy as jnp

def _softmax(x, axis=-1):
    return jax.nn.softmax(x, axis=axis)

def _gelu(x):
    return jax.nn.gelu(x, approximate=True)

def _silu(x):
    return jax.nn.silu(x)

def _sigmoid(x):
    return jax.nn.sigmoid(x)

def _layernorm(x, axis=-1, eps=1e-05):
    m = jnp.mean(x, axis=axis, keepdims=True)
    v = jnp.var(x, axis=axis, keepdims=True)
    return (x - m) / jnp.sqrt(v + eps)

def _scatter_add(tgt, idx, src, axis=0):
    return tgt.at[idx].add(src)

def _segment_sum(src, seg, n):
    return jax.ops.segment_sum(src, seg, n)
kernel_name = 'mk_seq_preln_d2_jaxref_r8_7c849b'

def setup_inputs(seed: int=0):
    np.random.seed(seed)
    _w = jnp.asarray

    def _L0_attn_setup():
        import jax, jax.numpy as jnp
        import numpy as np
        import math
        DIM = 512
        N_HEADS = 32
        N_KV_HEADS = 8
        HEAD_DIM = DIM // N_HEADS
        N_REP = N_HEADS // N_KV_HEADS
        ROPE_BASE = 10000.0

        def apply_rotary_emb(x):
            b, s, h, d = x.shape
            inv_freq = 1.0 / ROPE_BASE ** (jnp.arange(0, d, 2, dtype=jnp.float32) / d)
            pos = jnp.arange(s, dtype=jnp.float32)
            ang = pos[:, None] * inv_freq[None, :]
            cos = jnp.cos(ang)[None, :, None, :]
            sin = jnp.sin(ang)[None, :, None, :]
            xr = x.reshape(b, s, h, d // 2, 2)
            x0, x1 = (xr[..., 0], xr[..., 1])
            out = jnp.stack([x0 * cos - x1 * sin, x0 * sin + x1 * cos], axis=-1)
            return out.reshape(b, s, h, d)
        key = jax.random.key(seed)
        ks = jax.random.split(key, 5)
        sc = 1.0 / math.sqrt(DIM)
        return {'x': jax.random.normal(ks[0], (2, 256, DIM), dtype=jnp.float32), 'Wq': jax.random.normal(ks[1], (DIM, N_HEADS * HEAD_DIM), dtype=jnp.float32) * sc, 'Wk': jax.random.normal(ks[2], (DIM, N_KV_HEADS * HEAD_DIM), dtype=jnp.float32) * sc, 'Wv': jax.random.normal(ks[3], (DIM, N_KV_HEADS * HEAD_DIM), dtype=jnp.float32) * sc, 'Wo': jax.random.normal(ks[4], (N_HEADS * HEAD_DIM, DIM), dtype=jnp.float32) * sc}
    _L0_attn_in = _L0_attn_setup()

    def _L0_ffn_setup():
        import jax, jax.numpy as jnp
        import numpy as np
        IN_DIM = 512
        UNITS = 512
        EPS = 1e-06

        def _ternary_kernel(key):
            limit = np.sqrt(6.0 / (IN_DIM + UNITS))
            w = jax.random.uniform(key, (IN_DIM, UNITS), jnp.float32, -limit, limit)
            scale = jnp.mean(jnp.abs(w)) + EPS
            return jnp.clip(jnp.round(w / scale), -1.0, 1.0)
        key = jax.random.key(seed)
        kx, kw = jax.random.split(key)
        x = jax.random.normal(kx, (8, 256, IN_DIM), jnp.float32)
        kernel = _ternary_kernel(kw)
        bias = jnp.zeros((UNITS,), jnp.float32)
        return {'x': x, 'kernel': kernel, 'bias': bias}
    _L0_ffn_in = _L0_ffn_setup()

    def _L1_attn_setup():
        import jax, jax.numpy as jnp
        import numpy as np
        BATCH, SEQ, HIDDEN = (2, 512, 512)
        HEADS, HEAD_DIM, BLOCK = (32, 128, 32)
        LAYER_IDX, N_LAYERS = (1, 32)
        EPS = 1e-05

        def _decays():
            base = 1.0 / 2.0 ** (8.0 / HEADS)
            exponent = jnp.arange(HEADS, dtype=jnp.float32) + 1.0
            factor = 1.0 - LAYER_IDX / (N_LAYERS - 1 + 1e-05) + 1e-05
            slope = (base ** exponent * factor)[:, None, None]
            r = jnp.arange(BLOCK, dtype=jnp.float32) + 1.0
            q_decay = jnp.exp(-slope * r[:, None])
            k_decay = jnp.exp(-slope * (BLOCK - r)[:, None])
            diff = r[:, None] - r[None, :]
            diag = slope[None] * diff[None, None]
            diag = jnp.where(diag >= 0, -diag, -jnp.inf)
            diag_decay = jnp.exp(diag)
            block_decay = jnp.exp(-slope * BLOCK)
            return (q_decay, k_decay, diag_decay, block_decay)
        key = jax.random.key(seed)
        ks = jax.random.split(key, 5)
        s = 0.02
        return {'hidden_states': jax.random.normal(ks[0], (BATCH, SEQ, HIDDEN), jnp.float32), 'qkv_w': jax.random.normal(ks[1], (3 * HEADS * HEAD_DIM, HIDDEN), jnp.float32) * s, 'out_w': jax.random.normal(ks[2], (HIDDEN, HEADS * HEAD_DIM), jnp.float32) * s, 'gate_w': jax.random.normal(ks[3], (HEADS * HEAD_DIM, HIDDEN), jnp.float32) * s, 'norm_w': jnp.ones((HEADS * HEAD_DIM,), jnp.float32)}
    _L1_attn_in = _L1_attn_setup()

    def _L1_ffn_setup():
        import jax, jax.numpy as jnp
        import numpy as np
        RANKS = (8, 16, 32, 64)
        TOPK = 1
        SCALING = 1.0 / 4
        key = jax.random.key(seed)
        ks = jax.random.split(key, 7)
        D_IN, D_OUT, MAX_R, N_RANKS = (512, 512, 64, len(RANKS))
        B_, S_ = (4, 256)
        return {'hidden_states': jax.random.normal(ks[0], (B_, S_, D_IN), jnp.float32), 'W': jax.random.normal(ks[1], (D_OUT, D_IN), jnp.float32) * 0.02, 'b': jax.random.normal(ks[2], (D_OUT,), jnp.float32) * 0.02, 'A': jax.random.normal(ks[3], (MAX_R, D_IN), jnp.float32) * 0.02, 'B': jnp.zeros((D_OUT, MAX_R), jnp.float32) + jax.random.normal(ks[4], (D_OUT, MAX_R), jnp.float32) * 0.02, 'gate_w': jax.random.normal(ks[5], (N_RANKS, D_IN), jnp.float32) * 0.02, 'gate_b': jax.random.normal(ks[6], (N_RANKS,), jnp.float32) * 0.02}
    _L1_ffn_in = _L1_ffn_setup()
    _d = {'L0_attn_x': _L0_attn_in['x'], 'L0_attn_Wq': _L0_attn_in['Wq'], 'L0_attn_Wk': _L0_attn_in['Wk'], 'L0_attn_Wv': _L0_attn_in['Wv'], 'L0_attn_Wo': _L0_attn_in['Wo'], 'L0_ffn_kernel': _L0_ffn_in['kernel'], 'L0_ffn_bias': _L0_ffn_in['bias'], 'L1_attn_qkv_w': _L1_attn_in['qkv_w'], 'L1_attn_out_w': _L1_attn_in['out_w'], 'L1_attn_gate_w': _L1_attn_in['gate_w'], 'L1_attn_norm_w': _L1_attn_in['norm_w'], 'L1_ffn_W': _L1_ffn_in['W'], 'L1_ffn_b': _L1_ffn_in['b'], 'L1_ffn_A': _L1_ffn_in['A'], 'L1_ffn_B': _L1_ffn_in['B'], 'L1_ffn_gate_w': _L1_ffn_in['gate_w'], 'L1_ffn_gate_b': _L1_ffn_in['gate_b']}
    _x0 = _d['L0_attn_x']
    _d['L0_attn_x'] = jax.random.normal(jax.random.fold_in(jax.random.key(seed), 1), (2, 1024, 512), dtype=_x0.dtype)
    del _x0
    return _d

def reference(L0_attn_x, L0_attn_Wq, L0_attn_Wk, L0_attn_Wv, L0_attn_Wo, L0_ffn_kernel, L0_ffn_bias, L1_attn_qkv_w, L1_attn_out_w, L1_attn_gate_w, L1_attn_norm_w, L1_ffn_W, L1_ffn_b, L1_ffn_A, L1_ffn_B, L1_ffn_gate_w, L1_ffn_gate_b):

    def _L0_attn_ref(x, Wq, Wk, Wv, Wo):
        import jax, jax.numpy as jnp
        import numpy as np
        import math
        DIM = 512
        N_HEADS = 32
        N_KV_HEADS = 8
        HEAD_DIM = DIM // N_HEADS
        N_REP = N_HEADS // N_KV_HEADS
        ROPE_BASE = 10000.0

        def apply_rotary_emb(x):
            b, s, h, d = x.shape
            inv_freq = 1.0 / ROPE_BASE ** (jnp.arange(0, d, 2, dtype=jnp.float32) / d)
            pos = jnp.arange(s, dtype=jnp.float32)
            ang = pos[:, None] * inv_freq[None, :]
            cos = jnp.cos(ang)[None, :, None, :]
            sin = jnp.sin(ang)[None, :, None, :]
            xr = x.reshape(b, s, h, d // 2, 2)
            x0, x1 = (xr[..., 0], xr[..., 1])
            out = jnp.stack([x0 * cos - x1 * sin, x0 * sin + x1 * cos], axis=-1)
            return out.reshape(b, s, h, d)
        b, s, _ = x.shape
        xq = (x @ Wq).reshape(b, s, N_HEADS, HEAD_DIM)
        xk = (x @ Wk).reshape(b, s, N_KV_HEADS, HEAD_DIM)
        xv = (x @ Wv).reshape(b, s, N_KV_HEADS, HEAD_DIM)
        xq = apply_rotary_emb(xq)
        xk = apply_rotary_emb(xk)
        xk = jnp.repeat(xk, N_REP, axis=2)
        xv = jnp.repeat(xv, N_REP, axis=2)
        scores = jnp.einsum('bqhd,bkhd->bhqk', xq, xk) / math.sqrt(HEAD_DIM)
        causal = jnp.tril(jnp.ones((s, s), dtype=bool))
        scores = jnp.where(causal[None, None], scores, -jnp.inf)
        probs = jax.nn.softmax(scores.astype(jnp.float32), axis=-1).astype(xq.dtype)
        out = jnp.einsum('bhqk,bkhd->bqhd', probs, xv).reshape(b, s, N_HEADS * HEAD_DIM)
        return out @ Wo

    def _L0_ffn_ref(x, kernel, bias):
        import jax, jax.numpy as jnp
        import numpy as np
        IN_DIM = 512
        UNITS = 512
        EPS = 1e-06

        def _ternary_kernel(key):
            limit = np.sqrt(6.0 / (IN_DIM + UNITS))
            w = jax.random.uniform(key, (IN_DIM, UNITS), jnp.float32, -limit, limit)
            scale = jnp.mean(jnp.abs(w)) + EPS
            return jnp.clip(jnp.round(w / scale), -1.0, 1.0)
        return jnp.einsum('bsd,du->bsu', x, kernel) + bias

    def _L1_attn_ref(hidden_states, qkv_w, out_w, gate_w, norm_w):
        import jax, jax.numpy as jnp
        import numpy as np
        BATCH, SEQ, HIDDEN = (2, 512, 512)
        HEADS, HEAD_DIM, BLOCK = (32, 128, 32)
        LAYER_IDX, N_LAYERS = (1, 32)
        EPS = 1e-05

        def _decays():
            base = 1.0 / 2.0 ** (8.0 / HEADS)
            exponent = jnp.arange(HEADS, dtype=jnp.float32) + 1.0
            factor = 1.0 - LAYER_IDX / (N_LAYERS - 1 + 1e-05) + 1e-05
            slope = (base ** exponent * factor)[:, None, None]
            r = jnp.arange(BLOCK, dtype=jnp.float32) + 1.0
            q_decay = jnp.exp(-slope * r[:, None])
            k_decay = jnp.exp(-slope * (BLOCK - r)[:, None])
            diff = r[:, None] - r[None, :]
            diag = slope[None] * diff[None, None]
            diag = jnp.where(diag >= 0, -diag, -jnp.inf)
            diag_decay = jnp.exp(diag)
            block_decay = jnp.exp(-slope * BLOCK)
            return (q_decay, k_decay, diag_decay, block_decay)
        b, s, _ = hidden_states.shape
        h, d, bs = (HEADS, HEAD_DIM, BLOCK)
        nb = s // bs
        q_decay, k_decay, diag_decay, block_decay = _decays()
        qkv = jax.nn.silu(hidden_states @ qkv_w.T)
        qkv = qkv.reshape(b, s, h, 3, d)
        q = jnp.moveaxis(qkv[:, :, :, 0], 2, 1)
        k = jnp.moveaxis(qkv[:, :, :, 1], 2, 1)
        v = jnp.moveaxis(qkv[:, :, :, 2], 2, 1)

        def to_blocks(x):
            return jnp.moveaxis(x.reshape(b, h, nb, bs, d), 2, 0)
        qb, kb, vb = (to_blocks(q), to_blocks(k), to_blocks(v))

        def step(kv, blk):
            cq, ck, cv = blk
            scores = jnp.einsum('bhnd,bhmd->bhnm', cq, ck) * diag_decay
            intra = jnp.einsum('bhnm,bhmd->bhnd', scores, cv)
            inter = jnp.einsum('bhnd,bhde->bhne', cq * q_decay, kv)
            kv_next = kv * block_decay + jnp.einsum('bhnd,bhne->bhde', ck * k_decay, cv)
            return (kv_next, intra + inter)
        kv0 = jnp.zeros((b, h, d, d), hidden_states.dtype)
        _, out_blocks = jax.lax.scan(step, kv0, (qb, kb, vb))
        attn = jnp.moveaxis(out_blocks, 0, 2)
        attn = attn.reshape(b, h, s, d).transpose(0, 2, 1, 3).reshape(b, s, h * d)
        xf = attn.astype(jnp.float32)
        xf = xf * jax.lax.rsqrt(jnp.mean(xf * xf, axis=-1, keepdims=True) + EPS)
        normed = norm_w * xf.astype(attn.dtype)
        gate = jax.nn.sigmoid(hidden_states @ gate_w.T)
        return gate * normed @ out_w.T

    def _L1_ffn_ref(hidden_states, W, b, A, B, gate_w, gate_b):
        import jax, jax.numpy as jnp
        import numpy as np
        RANKS = (8, 16, 32, 64)
        TOPK = 1
        SCALING = 1.0 / 4
        bsz, seq, d_in = hidden_states.shape
        out = jnp.einsum('bsd,od->bso', hidden_states, W) + b
        x = hidden_states.reshape(-1, d_in)
        scores = x @ gate_w.T + gate_b
        probs = jax.nn.softmax(scores, axis=-1)
        routing_weights, selected = jax.lax.top_k(probs, TOPK)
        routing_weights = routing_weights / jnp.sum(routing_weights, axis=-1, keepdims=True)
        lora_outputs = jnp.stack([x @ A[:r, :].T @ B[:, :r].T for r in RANKS], axis=1)
        sel = jnp.take_along_axis(lora_outputs, selected[:, :, None], axis=1)
        final = jnp.sum(sel * routing_weights[:, :, None], axis=1)
        return out + final.reshape(bsz, seq, -1)
    x = L0_attn_x
    x = x + _L0_attn_ref(_layernorm(x, axis=-1), L0_attn_Wq, L0_attn_Wk, L0_attn_Wv, L0_attn_Wo)
    x = x + _L0_ffn_ref(_layernorm(x, axis=-1), L0_ffn_kernel, L0_ffn_bias)
    x = x + _L1_attn_ref(_layernorm(x, axis=-1), L1_attn_qkv_w, L1_attn_out_w, L1_attn_gate_w, L1_attn_norm_w)
    x = x + _L1_ffn_ref(_layernorm(x, axis=-1), L1_ffn_W, L1_ffn_b, L1_ffn_A, L1_ffn_B, L1_ffn_gate_w, L1_ffn_gate_b)
    return x

_drawn_inputs = setup_inputs


def setup_inputs(seed=0):
    import zlib

    import numpy as np

    out = dict(_drawn_inputs(seed))
    spreads = {'L0_ffn_bias': (0.0, 0.8), 'L1_attn_norm_w': (1.0, 0.6)}
    factors = {'L1_attn_gate_w': 7.758,
     'L1_ffn_b': 56.678,
     'L1_ffn_A': 8.0,
     'L1_ffn_B': 8.0,
     'L1_ffn_gate_w': 8.0,
     'L1_ffn_gate_b': 8.0}
    for name, (base, spread) in spreads.items():
        noise = np.random.default_rng([zlib.crc32(name.encode()), seed]).standard_normal(out[name].shape)
        drawn = base * np.exp(spread * noise) if base else spread * noise
        out[name] = jnp.asarray(drawn.astype(out[name].dtype))
    for name, factor in factors.items():
        out[name] = (out[name] * factor).astype(out[name].dtype)
    return out
```

```python
from contextlib import ExitStack

import concourse.bass as bass
from concourse import mybir

F32 = mybir.dt.float32
F32R = mybir.dt.float32r
BF16 = mybir.dt.bfloat16
F16 = mybir.dt.float16
ALU = mybir.AluOpType
ACT = mybir.ActivationFunctionType
AX_X = mybir.AxisListType.X

P = 128
BATCH, SEQ, DIM = 2, 1024, 512
TILES = BATCH * SEQ // P
SEQ_TILES = SEQ // P
KC = DIM // P
HEADS, KV_HEADS, HEAD_DIM = 32, 8, 16
REP = HEADS // KV_HEADS
EPS = 1e-5
Q_PARTS = (0, 0, 0, 1, 1, 2)
K_PARTS = (0, 1, 2, 0, 1, 0)
STACK = len(Q_PARTS) * HEAD_DIM
MAX_PARTS = 3
V_COLS = 3 * HEAD_DIM + 1
L1_HEADS, L1_DIM = 32, 128
L1_PAIR = 2
L1_RAW = 4
L1_BANKS = (2, 4, 2)


def passes(hi_lo_a, hi_lo_b):
    (ah, al), (bh, bl) = hi_lo_a, hi_lo_b
    return ((ah, bh), (al, bh), (ah, bl))


class Core:

    def __init__(self, nc, ctx):
        self.nc, self.ctx, self.owned = nc, ctx, []

    def sb(self, name, shape, dt=F32):
        return self.ctx.enter_context(self.nc.sbuf_tensor(name, shape, dt))

    def banks(self):
        return [self.ctx.enter_context(self.nc.psum_tensor(f"bank{n}", [P, 512], F32)) for n in range(8)]

    def sem(self, name):
        self.owned.append(self.ctx.enter_context(self.nc.semaphore(name)))
        return self.owned[-1]

    def sems(self, name, n):
        return [self.sem(f"{name}{i}") for i in range(n)]

    def credit(self, sems):
        with self.nc.Block() as block:
            @block.gpsimd
            def _(pool):
                for sem in sems:
                    pool.sem_inc(sem, 1)

    def clear(self):
        with self.nc.Block() as block:
            @block.gpsimd
            def _(pool):
                for sem in self.owned:
                    pool.sem_clear(sem)


CREDIT = 1


def gate(eng, sem, value, passed):
    eng.wait_ge(sem, value)
    eng.sem_inc(passed, 1)


def layernorm_scales(core, tag, stats, mu, rstd, stats_ready, tiles=slice(0, TILES)):
    nc = core.nc
    tmp = core.sb(f"ln_tmp_{tag}", [P, 4, tiles.stop - tiles.start])
    step = core.sem(f"ln_step_{tag}")
    root = core.sem(f"ln_root_{tag}")
    me, mo = stats[:, tiles, 1], stats[:, tiles, 4]
    ve, vo = stats[:, tiles, 2], stats[:, tiles, 5]
    a, b, var, r = (tmp[:, n, :] for n in range(4))

    def vector(dve):
        n = [0]

        def chain(ins):
            n[0] += 1
            ins.then_inc(step, 1)
            dve.wait_ge(step, n[0])

        stats_ready(dve)
        chain(dve.tensor_tensor(mu[:, tiles], me, mo, ALU.add))
        chain(dve.tensor_scalar(mu[:, tiles], mu[:, tiles], 0.5, None, ALU.mult))
        chain(dve.tensor_tensor(a, me, mo, ALU.subtract))
        chain(dve.tensor_scalar(a, a, 0.5, None, ALU.mult))
        chain(dve.tensor_tensor(a, a, a, ALU.mult))
        chain(dve.tensor_tensor(b, ve, vo, ALU.add))
        chain(dve.tensor_scalar(b, b, 1.0 / DIM, EPS, ALU.mult, ALU.add))
        chain(dve.tensor_tensor(var, a, b, ALU.add))
        dve.wait_ge(root, 1)
        chain(dve.reciprocal(r, a))
        chain(dve.tensor_tensor(b, r, r, ALU.mult))
        chain(dve.tensor_tensor(b, b, var, ALU.mult))
        chain(dve.tensor_scalar(b, b, -0.5, 1.5, ALU.mult, ALU.add))
        chain(dve.tensor_tensor(rstd[:, tiles], r, b, ALU.mult))

    def scalar(act):
        act.wait_ge(step, 8)
        nc.scalar.activation(a, var, ACT.Sqrt).then_inc(root, 1)

    return vector, scalar


def split_weight(core, tag, raw, hi, lo, loaded, count, ready):
    def scalar(eng):
        eng.wait_ge(loaded, count)
        for c in range(KC):
            core.nc.scalar.copy(hi[:, c, :], raw[:, c, :]).then_inc(ready[0], 1)

    def vector(eng):
        for c in range(KC):
            eng.wait_ge(ready[0], c + 1)
            eng.tensor_tensor(lo[:, c, :], raw[:, c, :], hi[:, c, :], ALU.subtract).then_inc(ready[1], 1)

    return scalar, vector


def project_qkv(nc, banks, x_dram, wq, wk, wv, cos_dram, sin_dram, X, VS, ident_f, ident_b, QT_dram, KT_dram,
                stackT, stored):
    with ExitStack() as ctx:
        core = Core(nc, ctx)
        QK = DIM + KV_HEADS * HEAD_DIM
        QKV = QK + KV_HEADS * HEAD_DIM
        STACKS = HEADS + KV_HEADS
        PER_BANK = 8
        GROUPS = STACKS // PER_BANK
        w_raw = core.sb("qkv_w_raw", [P, KC, QKV])
        w_hi = core.sb("qkv_w_hi", [P, KC, QKV], F32R)
        w_lo = core.sb("qkv_w_lo", [P, KC, QKV], F32R)
        cos = core.sb("rope_cos", [P, SEQ_TILES, HEAD_DIM])
        sin = core.sb("rope_sin", [P, SEQ_TILES, HEAD_DIM])
        stats = core.sb("qkv_stats", [P, TILES, 6])
        mu = core.sb("qkv_mu", [P, TILES])
        rstd = core.sb("qkv_rstd", [P, TILES])
        xn = core.sb("qkv_xn", [P, 2, DIM])
        xT_hi = core.sb("qkv_xT_hi", [P, 2, DIM], F32R)
        xT_lo = core.sb("qkv_xT_lo", [P, 2, DIM], F32R)
        raw = core.sb("qk_raw", [P, 2, QK])
        swapped = core.sb("qk_swapped", [P, 2, QK])
        rot = core.sb("qkv_rot", [P, 2, QKV])
        part = core.sb("qkv_part", [P, 3, 2, QKV], BF16)
        stack = core.sb("qk_stack", [P, 2, STACKS, STACK], BF16)
        ps_xT, (ps_q, ps_kv) = banks[0:2], banks[2:4]
        ps_st = [bank[:, :].bitcast(BF16) for bank in banks[4:8]]

        x_in = core.sems("qkv_x_in", 4)
        w_in = core.sem("qkv_w_in")
        tables_in = core.sem("qkv_tables_in")
        w_ready = core.sems("qkv_w_ready", 2)
        stats_done = core.sem("qkv_stats_done")
        normed = core.sem("qkv_normed")
        transposed = core.sem("qkv_transposed")
        hi_done = core.sem("qkv_hi_done")
        lo_done = core.sem("qkv_lo_done")
        projected = core.sem("qkv_projected")
        evacuated = core.sem("qkv_evacuated")
        swap_done = core.sem("qkv_swap_done")
        cos_done = core.sem("qkv_cos_done")
        rotated = core.sem("qkv_rotated")
        h_done = core.sem("qkv_h_done")
        r1_done = core.sem("qkv_r1_done")
        m_done = core.sem("qkv_m_done")
        l_done = core.sem("qkv_l_done")
        stacked = core.sem("qkv_stacked")
        stack_T = core.sem("stack_T")
        bank_by_act = core.sem("stack_bank_by_act")
        bank_by_dve = core.sem("stack_bank_by_dve")

        ACT_BANKS = (0, 2, 4)
        STACKINGS = 7

        def bank_free(eng, n):
            if n < 4:
                return
            t, g = divmod(n - 4, GROUPS)
            if g in ACT_BANKS:
                eng.wait_ge(bank_by_act, t * 3 + ACT_BANKS.index(g) + 1)
            else:
                eng.wait_ge(bank_by_dve, t * 2 + (1, 3).index(g) + 1)

        STARTS = (0, 4, 8, TILES)
        scales = {}
        for n, (first, last) in enumerate(zip(STARTS, STARTS[1:])):
            scales[first - 3 if first else -2] = (first, last, layernorm_scales(
                core, f"qkv{n}", stats, mu, rstd, lambda dve, last=last: dve.wait_ge(stats_done, last),
                slice(first, last)))
        w_scalar, w_vector = split_weight(core, "qkv", w_raw, w_hi, w_lo, w_in, 48, w_ready)

        def evacuate_stack(eng, copy, t, groups, done):
            for g in groups:
                n = t * GROUPS + g
                eng.wait_ge(stack_T, n + 1)
                if t % 2 == 0 and t >= 4:
                    eng.wait_ge(stored[(t // 2) % 2], 32 * (t // 4))
                copy(stackT[:, (t // 2) % 2, g * PER_BANK:(g + 1) * PER_BANK, t % 2, :],
                     ps_st[n % 4][0:STACK, :].rearrange("r (h q) -> r h q", h=PER_BANK)).then_inc(done, 1)

        with nc.Block() as block:
            @block.sync
            def _(sp):
                xv = x_dram.rearrange("b (t p) d -> p (b t) d", p=P)
                sp.dma_start(X[:, 0:4, :], xv[:, 0:4, :]).then_inc(x_in[0], 16)
                wv4 = [w.rearrange("(c p) n -> p c n", p=P) for w in (wq, wk, wv)]
                for w, a, b in zip(wv4, (0, DIM, QK), (DIM, QK, QKV)):
                    sp.dma_start(w_raw[:, :, a:b], w).then_inc(w_in, 16)
                sp.dma_start(cos[:, :, :], cos_dram).then_inc(tables_in, 16)
                sp.dma_start(sin[:, :, :], sin_dram).then_inc(tables_in, 16)
                for n in range(1, 4):
                    sp.dma_start(X[:, 4 * n:4 * n + 4, :], xv[:, 4 * n:4 * n + 4, :]).then_inc(x_in[n], 16)
                for pair in range(TILES // 2):
                    sp.wait_ge(bank_by_act, (2 * pair + 2) * 3)
                    sp.wait_ge(bank_by_dve, (2 * pair + 2) * 2)
                    b, q0 = divmod(pair, SEQ_TILES // 2)
                    src = stackT[:, pair % 2, :, :, :].rearrange("r h t q -> r h (t q)")
                    cols = slice(q0 * 2 * P, (q0 + 1) * 2 * P)
                    sp.dma_start(QT_dram[b * HEADS:(b + 1) * HEADS, :, cols].rearrange("h r q -> r h q"),
                                 src[:, 0:HEADS, :]).then_inc(stored[pair % 2], 16)
                    sp.dma_start(KT_dram[b * KV_HEADS:(b + 1) * KV_HEADS, :, cols].rearrange("h r q -> r h q"),
                                 src[:, HEADS:STACKS, :]).then_inc(stored[pair % 2], 16)

            @block.gpsimd
            def _(pool):
                nc.gpsimd.memset(VS[:, :, :, V_COLS - 1:V_COLS], 1.0)
                pool.wait_ge(tables_in, 32)
                for t in range(TILES):
                    s = t % 2
                    b, q = divmod(t, SEQ_TILES)
                    pool.wait_ge(evacuated, 3 * t + 3)
                    if t >= 2:
                        pool.wait_ge(rotated, t - 1)
                        pool.wait_ge(l_done, t - 1)
                    nc.gpsimd.tensor_tensor(
                        rot[:, s, 0:QK].rearrange("p (h d) -> p h d", d=HEAD_DIM),
                        raw[:, s, :].rearrange("p (h d) -> p h d", d=HEAD_DIM),
                        cos[:, q, :].unsqueeze(1).broadcast_to([P, STACKS, HEAD_DIM]), ALU.mult).then_inc(cos_done, 1)
                    rv = raw[:, s, :].rearrange("p (h f two) -> p h f two", f=8, two=2)
                    sv = swapped[:, s, :].rearrange("p (h f two) -> p h f two", f=8, two=2)
                    tv = sin[:, q, :].rearrange("p (f two) -> p f two", two=2)
                    for e in range(2):
                        nc.gpsimd.tensor_tensor(
                            sv[:, :, :, e], rv[:, :, :, 1 - e],
                            tv[:, :, e].unsqueeze(1).broadcast_to([P, STACKS, 8]), ALU.mult).then_inc(swap_done, 1)

            @block.scalar
            def _(act):
                scales[-2][2][1](act)
                w_scalar(act)
                for s in range(-1, TILES + 3):
                    if s >= 0 and s in scales:
                        scales[s][2][1](act)
                    t = s - 2
                    if 0 <= t < TILES:
                        act.wait_ge(rotated, t + 1)
                        if t >= 2:
                            act.wait_ge(stacked, STACKINGS * (t - 1))
                        nc.scalar.copy(part[:, 0, t % 2, :], rot[:, t % 2, :]).then_inc(h_done, 1)
                        act.wait_ge(r1_done, t + 1)
                        nc.scalar.copy(part[:, 1, t % 2, :], rot[:, t % 2, :]).then_inc(m_done, 1)
                    t = s
                    if 0 <= t < TILES:
                        act.wait_ge(projected, t + 1)
                        if t >= 2:
                            act.wait_ge(cos_done, t - 1)
                            act.wait_ge(swap_done, 2 * (t - 1))
                            act.wait_ge(l_done, t - 1)
                        nc.scalar.copy(raw[:, t % 2, 0:DIM], ps_q[:, :]).then_inc(evacuated, 1)
                        nc.scalar.copy(raw[:, t % 2, DIM:QK], ps_kv[:, 0:QK - DIM]).then_inc(evacuated, 1)
                        nc.scalar.copy(rot[:, t % 2, QK:QKV], ps_kv[:, QK - DIM:QKV - DIM]).then_inc(evacuated, 1)
                    t = s + 1
                    if t < TILES:
                        act.wait_ge(transposed, t + 1)
                        if t >= 2:
                            act.wait_ge(projected, t - 1)
                        nc.scalar.copy(xT_hi[:, t % 2, :], ps_xT[t % 2][:, :]).then_inc(hi_done, 1)
                    t = s - 3
                    if 0 <= t < TILES:
                        evacuate_stack(act, nc.scalar.copy, t, ACT_BANKS, bank_by_act)

            @block.vector
            def _(dve):
                def count_tiles(n):
                    dve.wait_ge(x_in[n], 16)
                    for t in range(4 * n, 4 * n + 4):
                        dve.bn_stats(stats[:, t, :], X[:, t, :]).then_inc(stats_done, 1)


                def normalize(t):
                    if t >= 2:
                        dve.wait_ge(transposed, t - 1)
                    dve.tensor_scalar(xn[:, t % 2, :], X[:, t, :], mu[:, t:t + 1], rstd[:, t:t + 1],
                                      ALU.subtract, ALU.mult).then_inc(normed, 1)

                count_tiles(0)
                scales[-2][2][0](dve)
                normalize(0)
                normalize(1)
                w_vector(dve)
                for s in range(-1, TILES + 4):
                    if s >= 0 and s in scales:
                        first, last, (ln_vector, _) = scales[s]
                        for n in range(first // 4, last // 4):
                            count_tiles(n)
                        ln_vector(dve)
                    t = s - 2
                    i = t % 2
                    chain = 0 <= t < TILES
                    if chain:
                        dve.wait_ge(cos_done, t + 1)
                        dve.wait_ge(swap_done, 2 * t + 2)
                        dve.tensor_tensor(rot[:, i, 0:QK], rot[:, i, 0:QK], swapped[:, i, :],
                                          ALU.add).then_inc(rotated, 1)
                    if 0 <= s and s + 2 < TILES:
                        normalize(s + 2)
                    if chain:
                        dve.wait_ge(rotated, t + 1)
                        dve.wait_ge(h_done, t + 1)
                        dve.tensor_tensor(rot[:, i, :], rot[:, i, :], part[:, 0, i, :], ALU.subtract).then_inc(r1_done, 1)
                    if 0 <= s - 4 < TILES:
                        evacuate_stack(dve, dve.tensor_copy, s - 4, (1, 3), bank_by_dve)
                    if chain:
                        dve.wait_ge(m_done, t + 1)
                        dve.wait_ge(r1_done, t + 1)
                        dve.tensor_tensor(part[:, 2, i, :], rot[:, i, :], part[:, 1, i, :], ALU.subtract).then_inc(l_done, 1)
                        dve.wait_ge(l_done, t + 1)
                        if t >= 2:
                            dve.wait_ge(stack_T, (t - 1) * GROUPS)
                        b, q = divmod(t, SEQ_TILES)
                        qst = stack[:, i, 0:HEADS, :].rearrange("p h (k d) -> p h k d", d=HEAD_DIM)
                        for n, first, count in ((0, 0, 3), (1, 3, 2), (2, 5, 1)):
                            src = part[:, n, i, 0:DIM].rearrange("p (h d) -> p h d", d=HEAD_DIM)
                            dve.tensor_copy(qst[:, :, first:first + count, :],
                                            src.unsqueeze(2).broadcast_to([P, HEADS, count, HEAD_DIM])
                                            ).then_inc(stacked, 1)
                        kst = stack[:, i, HEADS:STACKS, :].rearrange("p h (k d) -> p h k d", d=HEAD_DIM)
                        kv = part[:, :, i, DIM:QKV].rearrange("p n (h d) -> p h n d", d=HEAD_DIM)
                        for first, count in ((0, 3), (3, 2), (5, 1)):
                            dve.tensor_copy(kst[:, :, first:first + count, :],
                                            kv[:, 0:KV_HEADS, 0:count, :]).then_inc(stacked, 1)
                        vst = VS[:, b * KV_HEADS:(b + 1) * KV_HEADS, q, 0:3 * HEAD_DIM]
                        dve.tensor_copy(vst.rearrange("p h (n d) -> p h n d", d=HEAD_DIM),
                                        kv[:, KV_HEADS:2 * KV_HEADS, :, :]).then_inc(stacked, 1)
                    t = s + 1
                    if t < TILES:
                        dve.wait_ge(hi_done, t + 1)
                        if t >= 2:
                            dve.wait_ge(projected, t - 1)
                        dve.tensor_tensor(xT_lo[:, t % 2, :], ps_xT[t % 2][:, :], xT_hi[:, t % 2, :],
                                          ALU.subtract).then_inc(lo_done, 1)

            @block.tensor
            def _(pe):
                def transpose_x(t):
                    pe.wait_ge(normed, t + 1)
                    if t >= 2:
                        pe.wait_ge(lo_done, t - 1)
                    for c in range(KC):
                        mm = pe.transpose(ps_xT[t % 2][:, c * P:(c + 1) * P], xn[:, t % 2, c * P:(c + 1) * P],
                                          ident_f[:, :])
                    mm.then_inc(transposed, 1)

                transpose_x(0)
                pe.wait_ge(w_ready[1], KC)
                for s in range(TILES + 3):
                    t = s
                    if t < TILES:
                        pe.wait_ge(hi_done, t + 1)
                        pe.wait_ge(lo_done, t + 1)
                        if t >= 1:
                            pe.wait_ge(evacuated, 3 * t)
                        for ps, a, b in ((ps_q, 0, DIM), (ps_kv, DIM, QKV)):
                            n = 0
                            for x, w in passes((xT_hi, xT_lo), (w_hi, w_lo)):
                                for c in range(KC):
                                    mm = pe.matmul(ps[:, 0:b - a], x[:, t % 2, c * P:(c + 1) * P], w[:, c, a:b],
                                                   start=(n == 0), stop=(n == 3 * KC - 1))
                                    n += 1
                        mm.then_inc(projected, 1)
                    if s + 1 < TILES:
                        transpose_x(s + 1)
                    t = s - 3
                    if 0 <= t < TILES:
                        pe.wait_ge(stacked, STACKINGS * (t + 1))
                        for g in range(GROUPS):
                            n = t * GROUPS + g
                            bank_free(pe, n)
                            for h in range(PER_BANK):
                                mm = pe.transpose(ps_st[n % 4][0:STACK, h * P:(h + 1) * P],
                                                  stack[:, t % 2, g * PER_BANK + h, :], ident_b[:, :])
                            mm.then_inc(stack_T, 1)
        core.clear()


def softmax_attend(nc, banks, stored, prefetch, VS, O, QT_dram, KT_dram, ident_f, ident_b, mask_s, mask_t):
    with ExitStack() as ctx:
        core = Core(nc, ctx)
        UH = 16
        UG = UH // REP
        OH = P // HEAD_DIM
        TURNS = BATCH * HEADS // UH
        HALF = SEQ_TILES // 2
        UNIT = 4
        UNITS = [
            [(0, 0, 4)], [(1, 1, 3), (3, 3, 1)], [(0, 4, 4)], [(2, 2, 2), (6, 6, 2)],
            [(1, 4, 4)], [(2, 4, 4)], [(3, 4, 4)], [(4, 4, 4)], [(5, 5, 3), (7, 7, 1)],
        ]
        HALF_DONE = (3, 8)
        POOL_LO = (0, 1, 3, 4, 6, 7)
        NU = len(UNITS)
        SBANKS = [(q, h) for q in range(SEQ_TILES) for h in range(q // HALF + 1)]
        NS = len(SBANKS)
        S_AT = [SBANKS[NS * u // NU:NS * (u + 1) // NU] for u in range(NU)]
        SRING, RING = 3, 9
        LAG = 4
        MAX_AT = 5
        LO_LAG = 2
        SCALE = HEAD_DIM ** -0.5
        FU = UH * NU
        ST = UH * (NU + 1)
        ROWS = STACK + MAX_PARTS
        MP = MAX_PARTS * SEQ_TILES
        STEPS = 5

        QT = core.sb("att_QT", [ROWS, 4, SEQ], BF16)
        KT = core.sb("att_KT", [ROWS, 2, SEQ], BF16)
        V = core.sb("att_V", [P, 2, SEQ_TILES, V_COLS], BF16)
        expd = core.sb("att_exp", [P, RING, UNIT * P])
        e_hi = core.sb("att_e_hi", [P, RING, UNIT * P], F16)
        e_lo = core.sb("att_e_lo", [P, RING, UNIT * P], F16)
        mx = core.sb("att_max", [P, 2, SEQ_TILES])
        mx_2nd = core.sb("att_max_2nd", [P, 2, HALF])
        mx_rest = core.sb("att_max_rest", [P, 2, SEQ_TILES])
        mx_part = core.sb("att_max_part", [P, 2, MAX_PARTS, SEQ_TILES], BF16)
        mx_T = core.sb("att_max_T", [MP, 2, P], BF16)
        oT = core.sb("att_oT", [V_COLS, 2, HALF * P])
        o_sum = core.sb("att_o_sum", [P, SEQ_TILES, HEAD_DIM])
        o_den = core.sb("att_o_den", [P, SEQ_TILES, 1])
        ps_s, ps_t, ps_oT, ps_o = banks[0:SRING], banks[3:5], banks[5:7], banks[7]

        room = KC * DIM // (SEQ_TILES * P)
        w_raw = [O[:, room * n:room * (n + 1), :, :].rearrange("p a t n -> p (a t n)").rearrange(
            "p (c n) -> p c n", n=DIM) for n in range(len(prefetch))]
        w_in = core.sems("att_w_in", len(prefetch))
        w_split = core.sem("att_w_split")
        ones_set = core.sem("att_ones_set")
        q_in = core.sems("att_q_in", 4)
        k_in = core.sems("att_k_in", 2)
        v_in = core.sems("att_v_in", 2)
        max_in = core.sems("att_max_in", 2)
        s_ready = core.sem("att_s_ready")
        s_read = core.sems("att_s_read", SRING)
        max_step = core.sem("att_max_step")
        first_max = core.sem("att_first_max")
        t_ready = core.sem("att_t_ready")
        t_read = core.sems("att_t_read", 2)
        hi_ready = core.sem("att_hi_ready")
        lo_ready = core.sems("att_lo_ready", RING)
        pv_done = core.sems("att_pv_done", RING)
        oT_read = core.sems("att_oT_read", 2)
        o_ready = core.sem("att_o_ready")
        o_read = core.sem("att_o_read")
        o_step = core.sem("att_o_step")
        pe_passed = core.sem("att_pe_passed")
        dve_passed = core.sem("att_dve_passed")

        core.credit(pv_done + t_read + lo_ready + max_in + oT_read + [o_ready, o_read, o_step])

        def head_bank(j):
            return (NU + 1) * j + MAX_AT

        def unit_bank(j, u):
            return (NU + 1) * j + u + (u >= MAX_AT)

        def read_of(it, n):
            return ST // 2 * it + n // 2 + 1

        def ready_of(it, n):
            return ST * it + n + 2

        def slot_of(it, f):
            return FU // RING * it + f // RING

        def max_rows(n):
            return ps_t[n % 2][0:MP, 0:P // 2].bitcast(BF16)

        def max_columns(slot):
            return mx_part[:, slot, :, :].rearrange("p m q -> p (m q)")

        with nc.Block() as block:
            @block.sync
            def _(sp):
                def load_q(head, slot):
                    sp.dma_start(QT[0:STACK, slot, :], QT_dram[head]).then_inc(q_in[slot], 16)

                def load_kv(group, slot):
                    sp.dma_start(KT[0:STACK, slot, :], KT_dram[group]).then_inc(k_in[slot], 16)
                    sp.dma_start(V[:, slot, :, :], VS[:, group, :, :]).then_inc(v_in[slot], 16)

                def store_max(slot, qslot):
                    sp.dma_start(QT[STACK:ROWS, qslot, :].rearrange("m (q n) -> m q n", n=P),
                                 mx_T[:, slot, :]).then_inc(max_in[slot], 16)

                for g in range(2):
                    load_q(2 * g, 2 * g)
                    load_kv(g, g)
                    load_q(2 * g + 1, 2 * g + 1)
                for n, (weight, _, _) in enumerate(prefetch):
                    sp.dma_start(w_raw[n][:, :, :], weight.rearrange("(c p) n -> p c n", p=P)
                                 ).then_inc(w_in[n], 16)
                sp.wait_ge(first_max, 1)
                store_max(0, 0)
                for one in stored:
                    sp.wait_ge(one, 32 * TILES // 4)
                with sp.Fori(0, TURNS) as it:
                    nxt = (it + 1) % TURNS
                    for j in range(UH):
                        sp.wait_ge(t_read[head_bank(j) % 2], CREDIT + read_of(it, head_bank(j)))
                        store_max((j + 1) % 2, (j + 1) % 4)
                        sp.wait_ge(t_ready, ready_of(it, unit_bank(j, NU - 1)))
                        load_q(UH * it + j + 4 if j + 4 < UH else UH * nxt + j + 4 - UH, j % 4)
                        if j % REP == REP - 1:
                            last = NU * j + NU - 1
                            sp.wait_ge(pv_done[last % RING], CREDIT + slot_of(it, last) + 1)
                            g = j // REP
                            load_kv(UG * it + g + 2 if g + 2 < UG else UG * nxt + g + 2 - UG, g % 2)
                for group, n in ((q_in, UH // 4 * TURNS + 1), (k_in, UG // 2 * TURNS + 1),
                                 (v_in, UG // 2 * TURNS + 1)):
                    for one in group:
                        sp.wait_ge(one, 16 * n)
                for n in range(2):
                    sp.wait_ge(max_in[n], CREDIT + 16 * (TURNS * UH // 2 + 1 - n))

            @block.gpsimd
            def _(pool):
                for n, (_, w_hi, w_lo) in enumerate(prefetch):
                    for c in range(KC):
                        pool.wait_ge(w_split, KC * n + c + 1)
                        nc.gpsimd.tensor_tensor(w_lo[:, c, :], w_raw[n][:, c, :], w_hi[:, c, :], ALU.subtract)
                with pool.Fori(0, TURNS) as it:
                    for f in range(FU):
                        if f % NU in POOL_LO:
                            pool.wait_ge(hi_ready, FU * it + f + 1)
                            pool.wait_ge(pv_done[f % RING], CREDIT + slot_of(it, f))
                            nc.gpsimd.tensor_tensor(e_lo[:, f % RING, :], expd[:, f % RING, :],
                                                    e_hi[:, f % RING, :], ALU.subtract).then_inc(lo_ready[f % RING], 1)

            @block.scalar
            def _(act):
                def high_part(it, f):
                    j, u = divmod(f, NU)
                    n = unit_bank(j, u)
                    act.wait_ge(t_read[n % 2], CREDIT + read_of(it, n))
                    act.wait_ge(pv_done[f % RING], CREDIT + slot_of(it, f))
                    nc.scalar.copy(e_hi[:, f % RING, :], expd[:, f % RING, :]).then_inc(hi_ready, 1)

                def keep_oT(it, j):
                    f = NU * j + HALF_DONE[1]
                    act.wait_ge(pv_done[f % RING], CREDIT + slot_of(it, f) + 1)
                    act.wait_ge(o_ready, CREDIT + UH * it + j)
                    nc.scalar.copy(oT[:, 1, :], ps_oT[1][0:V_COLS, :]).then_inc(oT_read[1], 1)

                for n, (_, w_hi, _) in enumerate(prefetch):
                    act.wait_ge(w_in[n], 16)
                    for c in range(KC):
                        nc.scalar.copy(w_hi[:, c, :], w_raw[n][:, c, :]).then_inc(w_split, 1)
                act.wait_ge(t_ready, 1)
                nc.scalar.copy(mx_T[:, 0, :], max_rows(0)).then_inc(first_max, 1)
                with act.Fori(0, TURNS) as it:
                    for j in range(UH):
                        for u in range(NU):
                            if u == MAX_AT:
                                n = head_bank(j)
                                act.wait_ge(t_ready, ready_of(it, n))
                                act.wait_ge(max_in[(j + 1) % 2], CREDIT + 16 * (UH // 2 * it + (j + 1) // 2))
                                nc.scalar.copy(mx_T[:, (j + 1) % 2, :], max_rows(n)).then_inc(t_read[n % 2], 1)
                            f, n = NU * j + u, unit_bank(j, u)
                            act.wait_ge(t_ready, ready_of(it, n))
                            act.wait_ge(lo_ready[f % RING], CREDIT + slot_of(it, f))
                            nc.scalar.activation(expd[:, f % RING, :], ps_t[n % 2][:, :], ACT.Exp,
                                                 scale=SCALE).then_inc(t_read[n % 2], 1)
                            if f >= 1:
                                high_part(it, f - 1)
                            if j >= 1 and u == LAG:
                                keep_oT(it, j - 1)
                    high_part(it, FU - 1)
                    keep_oT(it, UH - 1)

            @block.vector
            def _(dve):
                dve.memset(KT[STACK:ROWS, :, :], -1.0).then_inc(ones_set, 1)

                def bank_max(it, k, n):
                    q, half = SBANKS[n]
                    width = min(512, (q + 1) * P - 512 * half)
                    to = mx_2nd[:, k % 2, q - HALF:q - HALF + 1] if half else mx[:, k % 2, q:q + 1]
                    dve.wait_ge(s_ready, NS * UH * it + NS * k + n + 1)
                    dve.tensor_reduce(to, ps_s[n % SRING][:, 0:width], AX_X, ALU.max).then_inc(s_read[n % SRING], 1)

                def max_parts(it, k, n):
                    slot, base = k % 2, STEPS * UH * it + STEPS * k
                    m, rest, part = mx[:, slot, :], mx_rest[:, slot, :], mx_part[:, slot, :, :]
                    if n == 0:
                        for one in s_read:
                            dve.wait_ge(one, NS // SRING * (UH * it + k + 1))
                        dve.tensor_tensor(mx[:, slot, HALF:], mx[:, slot, HALF:], mx_2nd[:, slot, :], ALU.max
                                          ).then_inc(max_step, 1)
                    if n in (1, 3):
                        gate(dve, max_step, base + n, dve_passed)
                        dve.tensor_copy(part[:, n // 2, :], m if n == 1 else rest).then_inc(max_step, 1)
                    if n in (2, 4):
                        dve.wait_ge(max_step, base + n)
                        dve.tensor_tensor(rest if n == 2 else part[:, 2, :], m if n == 2 else rest,
                                          part[:, n // 2 - 1, :], ALU.subtract).then_inc(max_step, 1)

                def low_part(it, f):
                    if f % NU in POOL_LO:
                        return
                    dve.wait_ge(hi_ready, FU * it + f + 1)
                    dve.wait_ge(pv_done[f % RING], CREDIT + slot_of(it, f))
                    dve.tensor_tensor(e_lo[:, f % RING, :], expd[:, f % RING, :], e_hi[:, f % RING, :],
                                      ALU.subtract).then_inc(lo_ready[f % RING], 1)

                def keep_oT(it, j):
                    f = NU * j + HALF_DONE[0]
                    gate(dve, pv_done[f % RING], CREDIT + slot_of(it, f) + 1, dve_passed)
                    gate(dve, o_ready, CREDIT + UH * it + j, dve_passed)
                    dve.tensor_copy(oT[:, 0, :], ps_oT[0][0:V_COLS, :]).then_inc(oT_read[0], 1)

                def finish_sums(it, j):
                    dve.wait_ge(o_ready, CREDIT + UH * it + j + 1)
                    dve.wait_ge(o_step, CREDIT + 2 * (UH * it + j))
                    acc = ps_o[:, 0:SEQ_TILES * V_COLS].rearrange("p (q c) -> p q c", c=V_COLS)
                    dve.tensor_reduce(o_sum[:, :, :],
                                      acc[:, :, 0:3 * HEAD_DIM].rearrange("p q (n d) -> p q d n", n=3),
                                      AX_X, ALU.add).then_inc(o_step, 1)
                    dve.reciprocal(o_den[:, :, :], acc[:, :, V_COLS - 1:V_COLS]).then_inc(o_read, 1)

                def finish(it, j):
                    dve.wait_ge(o_step, CREDIT + 2 * (UH * it + j) + 1)
                    dve.wait_ge(o_read, CREDIT + UH * it + j + 1)
                    dve.tensor_tensor(O[:, UH // OH * it + j // OH, :, j % OH * HEAD_DIM:(j % OH + 1) * HEAD_DIM], o_sum[:, :, :],
                                      o_den[:, :, :].broadcast_to([P, SEQ_TILES, HEAD_DIM]),
                                      ALU.mult).then_inc(o_step, 1)

                for k in range(2):
                    for n in range(NS):
                        bank_max(0, k, n)
                    if k == 0:
                        for step in range(STEPS):
                            max_parts(0, 0, step)
                with dve.Fori(0, TURNS) as it:
                    for j in range(UH):
                        dve.wait_ge(t_ready, ready_of(it, head_bank(j)) - (NU + 1) if j else ST * it + 1)
                        n = 0
                        for u in range(NU):
                            f = NU * j + u
                            if u < STEPS:
                                max_parts(it, j + 1, u)
                            if u == LAG + 3 and j >= 1:
                                finish_sums(it, j - 1)
                            if u == LAG + 4 and j >= 1:
                                finish(it, j - 1)
                            for _ in S_AT[u]:
                                bank_max(it, j + 2, n)
                                n += 1
                            if f >= LO_LAG:
                                low_part(it, f - LO_LAG)
                            if u == HALF_DONE[0] + LAG + 1:
                                keep_oT(it, j)
                    for f in range(FU - LO_LAG, FU):
                        low_part(it, f)
                    finish_sums(it, UH - 1)
                    finish(it, UH - 1)

            @block.tensor
            def _(pe):
                def scores_for_max(it, k, n):
                    q, half = SBANKS[n]
                    a, b = 512 * half, min(512 * (half + 1), (q + 1) * P)
                    diagonal = b == (q + 1) * P
                    slot = n % SRING
                    pe.wait_ge(s_read[slot], NS // SRING * (UH * it + k) + n // SRING)
                    mm = pe.matmul(ps_s[slot][:, 0:b - a], QT[0:STACK, k % 4, q * P:(q + 1) * P],
                                   KT[0:STACK, (k // REP) % 2, a:b], start=True, stop=not diagonal)
                    if diagonal:
                        mm = pe.matmul(ps_s[slot][:, b - a - P:b - a], ident_b[:, :], mask_s[:, :],
                                       start=False, stop=True)
                    mm.then_inc(s_ready, 1)

                def scores(it, j, u):
                    n = unit_bank(j, u)
                    if u == 0:
                        pe.wait_ge(max_in[j % 2], CREDIT + 16 * (UH // 2 * it + j // 2 + 1))
                    pe.wait_ge(t_read[n % 2], CREDIT + read_of(it, n) - 1)
                    a = 0
                    for key, q, count in UNITS[u]:
                        b = a + count * P
                        mm = pe.matmul(ps_t[n % 2][:, a:b], KT[:, (j // REP) % 2, key * P:(key + 1) * P],
                                       QT[:, j % 4, q * P:(q + count) * P], start=True, stop=key != q)
                        if key == q:
                            mm = pe.matmul(ps_t[n % 2][:, a:a + P], ident_b[:, :], mask_t[:, :],
                                           start=False, stop=True)
                        a = b
                    mm.then_inc(t_ready, 1)

                def times_v(it, f):
                    j, u = divmod(f, NU)
                    slot, group = f % RING, (j // REP) % 2
                    pe.wait_ge(lo_ready[slot], CREDIT + slot_of(it, f) + 1)
                    if j % REP == 0 and u == 0:
                        pe.wait_ge(v_in[group], 16 * (UG // 2 * it + j // REP // 2 + 1))
                    a = 0
                    for key, q, count in UNITS[u]:
                        half = q // HALF
                        if key == 0:
                            pe.wait_ge(oT_read[half], CREDIT + UH * it + j)
                        b, c = a + count * P, (q % HALF) * P
                        for part in (e_hi, e_lo):
                            mm = pe.matmul(ps_oT[half][0:V_COLS, c:c + b - a], V[:, group, key, :],
                                           part[:, slot, a:b], start=(key == 0 and part is e_hi),
                                           stop=(part is e_lo), skip_group_check=True)
                        a = b
                    mm.then_inc(pv_done[slot], 1)

                def turn_back(it, j):
                    for half in range(2):
                        gate(pe, oT_read[half], CREDIT + UH * it + j + 1, pe_passed)
                    gate(pe, o_read, CREDIT + UH * it + j, pe_passed)
                    for q in range(SEQ_TILES):
                        mm = pe.transpose(ps_o[:, q * V_COLS:(q + 1) * V_COLS],
                                          oT[:, q // HALF, (q % HALF) * P:(q % HALF + 1) * P],
                                          ident_f[0:V_COLS, 0:V_COLS])
                    mm.then_inc(o_ready, 1)

                pe.wait_ge(ones_set, 1)
                pe.wait_ge(k_in[0], 16)
                for k in range(2):
                    pe.wait_ge(q_in[k], 16)
                    for n in range(NS):
                        scores_for_max(0, k, n)
                pe.wait_ge(max_step, STEPS)
                pe.transpose(max_rows(0), max_columns(0), ident_b[:, :]).then_inc(t_ready, 1)
                pe.wait_ge(first_max, 1)
                with pe.Fori(0, TURNS) as it:
                    for j in range(UH):
                        k, n = j + 2, 0
                        for u in range(NU):
                            if u == MAX_AT:
                                m = head_bank(j)
                                pe.wait_ge(t_read[m % 2], CREDIT + read_of(it, m) - 1)
                                gate(pe, max_step, STEPS * (UH * it + j + 2), pe_passed)
                                pe.transpose(max_rows(m), max_columns((j + 1) % 2), ident_b[:, :]).then_inc(t_ready, 1)
                            scores(it, j, u)
                            if u == 0:
                                pe.wait_ge(q_in[k % 4], 16 * (UH // 4 * it + k // 4 + 1))
                                if k % REP == 0:
                                    pe.wait_ge(k_in[(k // REP) % 2], 16 * (UG // 2 * it + k // REP // 2 + 1))
                            for _ in S_AT[u]:
                                scores_for_max(it, k, n)
                                n += 1
                            if NU * j + u >= LAG:
                                times_v(it, NU * j + u - LAG)
                            if j >= 1 and u == LAG + 2:
                                turn_back(it, j - 1)
                    for f in range(FU - LAG, FU):
                        times_v(it, f)
                    turn_back(it, UH - 1)


def project_tiles(nc, banks, tag, X, w_hi, w_lo, ident_f, stats_out, source=None, stats_in=None, bias=None):
    with ExitStack() as ctx:
        core = Core(nc, ctx)
        xT_hi = core.sb(f"{tag}_xT_hi", [P, 2, DIM], F32R)
        xT_lo = core.sb(f"{tag}_xT_lo", [P, 2, DIM], F32R)
        ps_xT, ps_y = banks[0:2], banks[2:4]
        normed = core.sem(f"{tag}_normed")
        transposed = core.sem(f"{tag}_transposed")
        hi_done = core.sem(f"{tag}_hi_done")
        lo_done = core.sem(f"{tag}_lo_done")
        projected = core.sem(f"{tag}_projected")
        added = core.sem(f"{tag}_added")
        biased = core.sem(f"{tag}_biased")
        counted = core.sem(f"{tag}_counted")
        ln = source is None
        if ln:
            mu = core.sb(f"{tag}_mu", [P, TILES])
            rstd = core.sb(f"{tag}_rstd", [P, TILES])
            xn = core.sb(f"{tag}_xn", [P, 2, DIM])
            ln_vector, ln_scalar = layernorm_scales(core, tag, stats_in, mu, rstd, lambda dve: None)
            source = lambda t: xn[:, t % 2, :].rearrange("p (c n) -> p c n", n=P)
        if bias is not None:
            bias_all = core.sb(f"{tag}_bias", [P, DIM])
            bias_in = core.sem(f"{tag}_bias_in")

        with nc.Block() as block:
            @block.sync
            def _(sp):
                if bias is not None:
                    sp.dma_start(bias_all[:, :], bias.unsqueeze(0).broadcast_to([P, DIM])).then_inc(bias_in, 16)
                    sp.wait_ge(bias_in, 16)

            @block.gpsimd
            def _(pool):
                if bias is not None:
                    pool.wait_ge(bias_in, 16)
                    for t in range(TILES):
                        pool.wait_ge(added, t + 1)
                        nc.gpsimd.tensor_tensor(X[:, t, :], X[:, t, :], bias_all[:, :], ALU.add).then_inc(biased, 1)

            @block.scalar
            def _(act):
                if ln:
                    ln_scalar(act)
                for t in range(TILES):
                    act.wait_ge(transposed, t + 1)
                    if t >= 2:
                        act.wait_ge(projected, t - 1)
                    nc.scalar.copy(xT_hi[:, t % 2, :], ps_xT[t % 2][:, :]).then_inc(hi_done, 1)

            @block.vector
            def _(dve):
                if ln:
                    ln_vector(dve)

                def normalize(t):
                    if t >= 2:
                        dve.wait_ge(transposed, t - 1)
                    dve.tensor_scalar(xn[:, t % 2, :], X[:, t, :], mu[:, t:t + 1], rstd[:, t:t + 1],
                                      ALU.subtract, ALU.mult).then_inc(normed, 1)

                def count(t):
                    dve.wait_ge(biased if bias is not None else added, t + 1)
                    dve.bn_stats(stats_out[:, t, :], X[:, t, :]).then_inc(counted, 1)

                for s in range(-2, TILES + 2):
                    if ln and s + 2 < TILES:
                        normalize(s + 2)
                    if 0 <= s + 1 < TILES:
                        t = s + 1
                        dve.wait_ge(hi_done, t + 1)
                        if t >= 2:
                            dve.wait_ge(projected, t - 1)
                        dve.tensor_tensor(xT_lo[:, t % 2, :], ps_xT[t % 2][:, :], xT_hi[:, t % 2, :],
                                          ALU.subtract).then_inc(lo_done, 1)
                    if 0 <= s - 1 < TILES:
                        t = s - 1
                        dve.wait_ge(projected, t + 1)
                        if ln:
                            dve.wait_ge(normed, t + 1)
                        dve.tensor_tensor(X[:, t, :], X[:, t, :], ps_y[t % 2][:, :], ALU.add).then_inc(added, 1)
                    if 0 <= s - 2 < TILES:
                        count(s - 2)

            @block.tensor
            def _(pe):
                def transpose_x(t):
                    if ln:
                        pe.wait_ge(normed, t + 1)
                    if t >= 2:
                        pe.wait_ge(lo_done, t - 1)
                    for c in range(KC):
                        mm = pe.transpose(ps_xT[t % 2][:, c * P:(c + 1) * P], source(t)[:, c, :], ident_f[:, :])
                    mm.then_inc(transposed, 1)

                transpose_x(0)
                transpose_x(1)
                for t in range(TILES):
                    pe.wait_ge(lo_done, t + 1)
                    if t >= 2:
                        pe.wait_ge(added, t - 1)
                    n = 0
                    for x, w in passes((xT_hi, xT_lo), (w_hi, w_lo)):
                        for c in range(KC):
                            mm = pe.matmul(ps_y[t % 2][:, :], x[:, t % 2, c * P:(c + 1) * P], w[:, c, :],
                                           start=(n == 0), stop=(n == 3 * KC - 1))
                            n += 1
                    mm.then_inc(projected, 1)
                    if t + 2 < TILES:
                        transpose_x(t + 2)


def normalize_transposed(core, ps_xT, b, X, mu, rstd, xn, xT_hi, xT_lo, stats, ident_f, lo_done):
    tag = f"l1n{b}"
    nc = core.nc
    normed = core.sem(f"{tag}_normed")
    transposed = core.sem(f"{tag}_transposed")
    hi_done = core.sem(f"{tag}_hi_done")
    ln_vector, ln_scalar = layernorm_scales(core, tag, stats, mu, rstd, lambda dve: None)

    def scalar(act):
        ln_scalar(act)
        for t in range(SEQ_TILES):
            act.wait_ge(transposed, t + 1)
            nc.scalar.copy(xT_hi[:, :, t * P:(t + 1) * P],
                           ps_xT[t % 4][:, :].rearrange("p (c n) -> p c n", n=P)).then_inc(hi_done, 1)

    def vector(dve):
        ln_vector(dve)
        for s in range(SEQ_TILES + 1):
            if s < SEQ_TILES:
                t = SEQ_TILES * b + s
                if s >= 2:
                    dve.wait_ge(transposed, s - 1)
                dve.tensor_scalar(xn[:, s % 2, :], X[:, t, :], mu[:, t:t + 1], rstd[:, t:t + 1],
                                  ALU.subtract, ALU.mult).then_inc(normed, 1)
            if s >= 1:
                t = s - 1
                dve.wait_ge(hi_done, t + 1)
                dve.tensor_tensor(xT_lo[:, :, t * P:(t + 1) * P],
                                  ps_xT[t % 4][:, :].rearrange("p (c n) -> p c n", n=P),
                                  xT_hi[:, :, t * P:(t + 1) * P], ALU.subtract).then_inc(lo_done, 1)

    def tensor(pe):
        for t in range(SEQ_TILES):
            pe.wait_ge(normed, t + 1)
            if t >= 4:
                pe.wait_ge(lo_done, t - 3)
            for c in range(KC):
                mm = pe.transpose(ps_xT[t % 4][:, c * P:(c + 1) * P], xn[:, t % 2, c * P:(c + 1) * P],
                                  ident_f[:, :])
            mm.then_inc(transposed, 1)

    return scalar, vector, tensor


def linear_attend_buffers(core, kT, qd):
    w_raw = core.sb("l1_w_raw", [P, L1_RAW, DIM])
    o_raw = core.sb("l1_o_raw", [P, KC, L1_PAIR * P])
    w_T = [core.sb(f"l1_w_T{n}", [P, 3, L1_PAIR, KC, P], F32R) for n in range(2)]
    v_T = [core.sb(f"l1_v_T{n}", [P, KC, L1_PAIR, P], F32R) for n in range(2)]
    o_T = [core.sb(f"l1_o_T{n}", [P, L1_PAIR, DIM], F32R) for n in range(2)]
    qT = core.sb("l1_qT", [P, L1_PAIR, SEQ])
    gT = core.sb("l1_gT", [P, L1_PAIR, SEQ])
    v = core.sb("l1_v", [P, SEQ_TILES, L1_PAIR * P])
    kd = core.sb("l1_kd", [P, SEQ])
    sc = core.sb("l1_sc", [P, SEQ])
    state = core.sb("l1_state", [P, SEQ_TILES, P])
    y_hi = core.sb("l1_y_hi", [P, L1_PAIR, SEQ], F32R)
    y_lo = core.sb("l1_y_lo", [P, L1_PAIR, SEQ], F32R)
    sq = core.sb("l1_sq", [P, 512])
    sq_sum = core.sb("l1_sq_sum", [P, SEQ])
    acc = core.sb("l1_acc", [P, SEQ_TILES, DIM])
    mask = core.sb("l1_mask", [P, L1_PAIR, P])
    q_decay = core.sb("l1_q_decay", [P, L1_PAIR, P])
    scales = core.sb("l1_scales", [P, L1_PAIR, 2])
    norm = core.sb("l1_norm", [P, L1_PAIR])
    ones = core.sb("l1_ones", [P, 1])
    rms = core.sb("l1_rms", [P, 4, SEQ_TILES])
    return (w_raw, o_raw, w_T, v_T, o_T, qT, kT, gT, v, qd, kd, sc, state, y_hi, y_lo, sq, sq_sum, acc, mask, q_decay,
            scales, norm, ones, rms)


def linear_attend_semaphores(core):
    w_in = core.sems("l1_w_in", L1_RAW)
    o_in = core.sem("l1_o_in")
    const_in = core.sem("l1_const_in")
    p_ready = core.sem("l1_p_ready")
    p_read = core.sems("l1_p_read", L1_BANKS[0])
    a_ready = core.sem("l1_a_ready")
    a_read = core.sems("l1_a_read", L1_BANKS[1])
    y_ready = core.sem("l1_y_ready")
    y_read = core.sems("l1_y_read", L1_BANKS[2])
    fill_hi = core.sem("l1_fill_hi")
    qd_ready = core.sem("l1_qd_ready")
    state_ready = core.sem("l1_state_ready")
    sq_ready = core.sem("l1_sq_ready")
    sq_added = core.sem("l1_sq_added")
    yhi_ready = core.sem("l1_yhi_ready")
    ylo_ready = core.sem("l1_ylo_ready")
    cleared = core.sem("l1_cleared")
    sum_ready = core.sem("l1_sum_ready")
    rms_step = core.sem("l1_rms_step")
    root = core.sem("l1_root")
    added = core.sem("l1_added")
    counted = core.sem("l1_counted")
    core.credit(a_read + y_read + [a_ready, y_ready, qd_ready, ylo_ready, sq_added])
    return (w_in, o_in, const_in, p_ready, p_read, a_ready, a_read, y_ready, y_read, fill_hi, qd_ready, state_ready,
            sq_ready, sq_added, yhi_ready, ylo_ready, cleared, sum_ready, rms_step, root, added, counted)


def linear_attend(nc, banks, buffers, sems, b, X, mu, rstd, xT_hi, xT_lo, qkv_w, out_w, gate_w, norm_w, decay,
                  q_decay_dram, scales_dram, stats_in, stats_out, ident_f, next_loads):
    tag = f"l1a{b}"
    with ExitStack() as ctx:
        core = Core(nc, ctx)
        HP = L1_PAIR
        TURNS = L1_HEADS // HP
        DONE = TURNS * (b + 1)
        C = SEQ_TILES
        H = SEQ // 512
        CH = C // H
        KINDS = ("q", "k", "v", "g")
        ROW_FILLS = len(KINDS) * HP
        FILLS = ROW_FILLS + HP
        RAW = L1_RAW

        def two(kind, h):
            return [(kind, h, 0), (kind, h, 1)]

        ORDER = ([("v", t) for t in range(C)] + two("k", 0) + two("q", 0) + two("g", 0)
                 + two("turn_k", 0) + [("k", 1, 0)] + two("score", 0) + [("k", 1, 1)] + two("update", 0)
                 + [("q", 1, 0), ("out", 0, 0), ("q", 1, 1), ("out", 0, 1)]
                 + two("turn_k", 1) + [("g", 1, 0)] + two("score", 1) + [("fill", 0), ("fill", 1)]
                 + two("update", 1) + [("g", 1, 1), ("fill", 2), ("fill", 3), ("out", 1, 0), ("fill", 4), ("fill", 5),
                                       ("out", 1, 1), ("fill", 6), ("fill", 7)]
                 + [("project", t) for t in range(C)] + [("fill", n) for n in range(ROW_FILLS, FILLS)])
        FILLS_IN_A = (3, 5, 8, 9)
        IN_P = [e for e in ORDER if e[0] in ("v", "q", "k", "g") or e[0] == "fill" and e[1] not in FILLS_IN_A]
        IN_A = [e for e in ORDER if e[0] in ("turn_k", "score", "update", "out")
                or e[0] == "fill" and e[1] in FILLS_IN_A]
        NP_, NA, NY = L1_BANKS
        RMS_STEPS = 6
        PR, LA = len(IN_P), len(IN_A)
        assert PR % NP_ == 0 and LA % NA == 0 and FILLS % NP_ == 0

        (w_raw, o_raw, w_T, v_T, o_T, qT, kT, gT, v, qd, kd, sc, state, y_hi, y_lo, sq, sq_sum, acc, mask, q_decay,
         scales, norm, ones, rms) = buffers
        ps_p, ps_a, ps_y = banks[0:NP_], banks[NP_:NP_ + NA], banks[NP_ + NA:]

        (w_in, o_in, const_in, p_ready, p_read, a_ready, a_read, y_ready, y_read, fill_hi, qd_ready, state_ready,
         sq_ready, sq_added, yhi_ready, ylo_ready, cleared, sum_ready, rms_step, root, added, counted) = sems

        lo_done = core.sem(f"{tag}_lo_done")
        n_scalar, n_vector, n_tensor = normalize_transposed(
            core, ps_a, b, X, mu, rstd, gT[:, :, 0:DIM], xT_hi, xT_lo, stats_in, ident_f, lo_done)

        def p_count(it, n):
            return FILLS + PR * it + n + 1

        def p_reads(it, n):
            return PR // NP_ * it + FILLS // NP_ + n // NP_ + 1

        def a_count(it, n):
            return LA * it + n + 1

        def a_reads(it, n):
            return LA // NA * it + n // NA + 1

        def wait_evacuated(eng, it, event):
            if event in IN_P:
                n = IN_P.index(event)
                eng.wait_ge(p_read[n % NP_], p_reads(it, n))
            else:
                n = IN_A.index(event)
                eng.wait_ge(a_read[n % NA], CREDIT + a_reads(it, n))

        def half(h):
            return slice(512 * h, 512 * h + 512)

        def chunk(c):
            return slice(P * c, P * c + P)

        def gated(h, s):
            return H * h + s

        def fill_target(parts, n):
            wt, vt, ot = parts
            if n >= ROW_FILLS:
                return ot[:, n - ROW_FILLS, :].rearrange("p (c n) -> p c n", n=P)
            h, kind = divmod(n, len(KINDS))
            if KINDS[kind] == "v":
                return vt[:, :, h, :]
            return wt[:, "qkg".index(KINDS[kind]), h, :, :]

        def fill_bank(bank):
            return bank[:, :].rearrange("p (c n) -> p c n", n=P)

        T_hi, T_lo = (w_T[0], v_T[0], o_T[0]), (w_T[1], v_T[1], o_T[1])
        qkv_v = qkv_w.rearrange("(g h k p) d -> g h k p d", h=HP, k=3, p=P)
        gate_v = gate_w.rearrange("(g h p) d -> g h p d", h=HP, p=P)
        out_v = out_w.rearrange("(c p) (g n) -> g p c n", p=P, n=HP * P)
        norm_v = norm_w.rearrange("(g h p) -> g p h", h=HP, p=P)

        with nc.Block() as block:
            @block.sync
            def _(sp):
                def load_raw(turn, n):
                    h, kind = divmod(n, len(KINDS))
                    src = gate_v[turn, h] if KINDS[kind] == "g" else qkv_v[turn, h, kind]
                    sp.dma_start(w_raw[:, n % RAW, :], src).then_inc(w_in[n % RAW], 16)

                def load_weights(turn, before, first=False):
                    for n in range(ROW_FILLS):
                        if n >= RAW:
                            sp.wait_ge(fill_hi, before + n - RAW + 1)
                        elif not first:
                            sp.wait_ge(fill_hi, before - FILLS + n + RAW + 1)
                        load_raw(turn, n)
                    if not first:
                        sp.wait_ge(fill_hi, before)
                    sp.dma_start(o_raw[:, :, :], out_v[turn]).then_inc(o_in, 16)

                if b == 0:
                    load_weights(0, 0, first=True)
                with sp.Fori(TURNS * b, TURNS * (b + 1)) as it:
                    sp.wait_ge(ylo_ready, CREDIT + HP * H * it)
                    sp.dma_start(mask[:, :, :], decay[it % TURNS].rearrange("h m n -> m h n")).then_inc(const_in, 16)
                    sp.dma_start(q_decay[:, :, :], q_decay_dram[it % TURNS].unsqueeze(0).broadcast_to([P, HP, P])
                                 ).then_inc(const_in, 16)
                    sp.dma_start(scales[:, :, :], scales_dram[it % TURNS]).then_inc(const_in, 16)
                    with nc.allow_non_contiguous_dma("a head's norm weights, one to a partition"):
                        sp.dma_start(norm[:, :], norm_v[it % TURNS]).then_inc(const_in, 16)
                    load_weights((it + 1) % TURNS, FILLS * it + FILLS)
                if next_loads:
                    sp.wait_ge(a_ready, CREDIT + LA * DONE)
                    to_and_from, loaded = next_loads
                    for to, src in to_and_from:
                        sp.dma_start(to, src).then_inc(loaded, 16)
                sp.wait_ge(o_in, 16 * (DONE + 1))
                sp.wait_ge(const_in, 64 * DONE)
                for s in w_in:
                    sp.wait_ge(s, 16 * ROW_FILLS // RAW * (DONE + 1))

            @block.gpsimd
            def _(pool):
                nc.gpsimd.memset(sq_sum[:, :], 0.0).then_inc(cleared, 1)
                if b:
                    pool.wait_ge(added, C * b)
                nc.gpsimd.memset(acc[:, :, :], 0.0).then_inc(cleared, 1)
                nc.gpsimd.memset(ones[:, :], 1.0).then_inc(cleared, 1)
                pool.wait_ge(cleared, 3 * b + 3)
                with pool.Fori(TURNS * b, TURNS * (b + 1)) as it:
                    for event in ORDER:
                        kind = event[0]
                        if kind == "q" and event[2] == 1:
                            h = event[1]
                            pool.wait_ge(const_in, 64 * it + 64)
                            for s in range(H):
                                wait_evacuated(pool, it, ("q", h, s))
                            pool.wait_ge(a_ready, CREDIT + (a_count(it, IN_A.index(("out", 0, 1))) if h else LA * it))
                            nc.gpsimd.tensor_tensor(
                                qd[:, :].rearrange("p (c n) -> p c n", n=P),
                                qT[:, h, :].rearrange("p (c n) -> p c n", n=P),
                                q_decay[:, h, :].unsqueeze(1).broadcast_to([P, C, P]), ALU.mult).then_inc(qd_ready, 1)
                        if kind == "out":
                            n = gated(*event[1:])
                            pool.wait_ge(sq_ready, HP * H * it + n + 1)
                            pool.wait_ge(sq_added, CREDIT + HP * H * it + n)
                            nc.gpsimd.tensor_tensor(sq_sum[:, half(event[2])], sq_sum[:, half(event[2])], sq[:, :],
                                                    ALU.add).then_inc(sq_added, 1)

            @block.scalar
            def _(act):
                def keep_fill(n, bank):
                    nc.scalar.copy(fill_target(T_hi, n), fill_bank(bank)).then_inc(fill_hi, 1)

                def high_y(it, h, s):
                    n = IN_A.index(("out", h, s))
                    act.wait_ge(a_read[n % NA], CREDIT + a_reads(it, n))
                    act.wait_ge(y_ready, CREDIT + C * it)
                    nc.scalar.copy(y_hi[:, h, half(s)], gT[:, h, half(s)]).then_inc(yhi_ready, 1)

                n_scalar(act)
                for n in range(FILLS if b == 0 else 0):
                    act.wait_ge(p_ready, n + 1)
                    keep_fill(n, ps_p[n % NP_])
                with act.Fori(TURNS * b, TURNS * (b + 1)) as it:
                    owed = None
                    for event in ORDER:
                        kind = event[0]
                        if event in IN_P:
                            n = IN_P.index(event)
                            act.wait_ge(p_ready, p_count(it, n))
                            if kind == "fill":
                                keep_fill(event[1], ps_p[n % NP_])
                            else:
                                if kind == "v":
                                    to, src, func = v[:, event[1], :], ps_p[n % NP_][:, 0:HP * P], ACT.Silu
                                else:
                                    dst = {"q": qT, "k": kT, "g": gT}[kind]
                                    to, src = dst[:, event[1], half(event[2])], ps_p[n % NP_][:, :]
                                    func = ACT.Sigmoid if kind == "g" else ACT.Silu
                                    if kind == "q":
                                        act.wait_ge(qd_ready, CREDIT + HP * it)
                                    if kind == "g":
                                        act.wait_ge(ylo_ready, CREDIT + HP * H * it)
                                nc.scalar.activation(to, src, func).then_inc(p_read[n % NP_], 1)
                        if kind in ("turn_k", "out") or kind == "fill" and event in IN_A:
                            n = IN_A.index(event)
                            act.wait_ge(a_ready, CREDIT + a_count(it, n))
                            if kind == "fill":
                                keep_fill(event[1], ps_a[n % NA])
                        if kind == "turn_k":
                            act.wait_ge(const_in, 64 * it + 64)
                            nc.scalar.mul(kd[:, half(event[2])], ps_a[n % NA][:, :], scales[:, event[1], 0:1]
                                          ).then_inc(a_read[n % NA], 1)
                        if owed:
                            high_y(it, *owed)
                            owed = None
                        if kind == "out":
                            act.wait_ge(sq_added, CREDIT + HP * H * it + gated(*event[1:]))
                            nc.scalar.activation(sq[:, :], ps_a[n % NA][:, :], ACT.Square).then_inc(sq_ready, 1)
                            owed = event[1:]
                act.wait_ge(rms_step, RMS_STEPS * b + 1)
                nc.scalar.activation(rms[:, 1, :], rms[:, 0, :], ACT.Sqrt).then_inc(root, 1)

            @block.vector
            def _(dve):
                def low_fill(n, count, bank, bank_read):
                    dve.wait_ge(fill_hi, count)
                    dve.tensor_tensor(fill_target(T_lo, n), fill_bank(bank), fill_target(T_hi, n),
                                      ALU.subtract).then_inc(bank_read, 1)

                def low_y(it, h, s):
                    dve.wait_ge(yhi_ready, HP * H * it + gated(h, s) + 1)
                    dve.wait_ge(y_ready, CREDIT + C * it)
                    dve.tensor_tensor(y_lo[:, h, half(s)], gT[:, h, half(s)], y_hi[:, h, half(s)],
                                      ALU.subtract).then_inc(ylo_ready, 1)

                def add_to_x(b):
                    r = rms[:, 2, :]
                    for t in range(C):
                        x = X[:, C * b + t, :]
                        dve.scalar_tensor_tensor(x, acc[:, t, :], r[:, t:t + 1], x, ALU.mult, ALU.add
                                                 ).then_inc(added, 1)
                    for t in range(C):
                        dve.wait_ge(added, C * b + t + 1)
                        dve.bn_stats(stats_out[:, C * b + t, :], X[:, C * b + t, :]).then_inc(counted, 1)

                n_vector(dve)
                if b:
                    add_to_x(b - 1)
                for n in range(FILLS if b == 0 else 0):
                    low_fill(n, n + 1, ps_p[n % NP_], p_read[n % NP_])
                dve.wait_ge(cleared, 3 * b + 3)
                with dve.Fori(TURNS * b, TURNS * (b + 1)) as it:
                    owed = None
                    for event in ORDER:
                        kind = event[0]
                        if kind == "fill":
                            if event in IN_P:
                                n = IN_P.index(event)
                                bank, bank_read = ps_p[n % NP_], p_read[n % NP_]
                            else:
                                n = IN_A.index(event)
                                bank, bank_read = ps_a[n % NA], a_read[n % NA]
                            low_fill(event[1], FILLS * it + FILLS + event[1] + 1, bank, bank_read)
                        if kind == "score":
                            _, h, s = event
                            n = IN_A.index(event)
                            dve.wait_ge(a_ready, CREDIT + a_count(it, n))
                            dve.wait_ge(const_in, 64 * it + 64)
                            dve.tensor_tensor(sc[:, half(s)].rearrange("p (c n) -> p c n", n=P),
                                              ps_a[n % NA][:, :].rearrange("p (c n) -> p c n", n=P),
                                              mask[:, h, :].unsqueeze(1).broadcast_to([P, CH, P]),
                                              ALU.mult).then_inc(a_read[n % NA], 1)
                        if kind == "update":
                            _, h, s = event
                            n = IN_A.index(event)
                            dve.wait_ge(a_ready, CREDIT + a_count(it, n))
                            for c in range(CH * s, CH * s + CH):
                                if c == C - 1:
                                    break
                                src = ps_a[n % NA][:, chunk(c % CH)]
                                if c == 0:
                                    ins = dve.tensor_copy(state[:, 1, :], src)
                                else:
                                    dve.wait_ge(state_ready, (C - 1) * (HP * it + h) + c)
                                    ins = dve.scalar_tensor_tensor(state[:, c + 1, :], state[:, c, :],
                                                                   scales[:, h, 1:2], src, ALU.mult, ALU.add)
                                ins.then_inc(state_ready, 1)
                            dve.wait_ge(state_ready, (C - 1) * (HP * it + h) + min(CH * s + CH, C - 1))
                            dve.sem_inc(a_read[n % NA], 1)
                        if owed and kind in ("out", "fill", "project"):
                            low_y(it, *owed)
                            owed = None
                        if kind == "out":
                            _, h, s = event
                            n = IN_A.index(event)
                            dve.wait_ge(sq_ready, HP * H * it + gated(h, s) + 1)
                            wait_evacuated(dve, it, ("g", h, s))
                            dve.scalar_tensor_tensor(gT[:, h, half(s)], ps_a[n % NA][:, :], norm[:, h:h + 1],
                                                     gT[:, h, half(s)], ALU.mult, ALU.mult).then_inc(a_read[n % NA], 1)
                            owed = event[1:]
                        if kind == "project":
                            t = event[1]
                            dve.wait_ge(y_ready, CREDIT + C * it + t + 1)
                            dve.wait_ge(y_read[t % NY], CREDIT + C // NY * it + t // NY)
                            if t < NY:
                                for other in y_read:
                                    dve.wait_ge(other, CREDIT + C // NY * it)
                            dve.tensor_tensor(acc[:, t, :], acc[:, t, :], ps_y[t % NY][:, :], ALU.add
                                              ).then_inc(y_read[t % NY], 1)
                for other in y_read:
                    dve.wait_ge(other, CREDIT + C // NY * DONE)
                step = [RMS_STEPS * b]

                def chain(ins):
                    step[0] += 1
                    ins.then_inc(rms_step, 1)
                    dve.wait_ge(rms_step, step[0])

                var, r, t1 = rms[:, 0, :], rms[:, 2, :], rms[:, 3, :]
                dve.wait_ge(sum_ready, b + 1)
                chain(dve.tensor_scalar(var, ps_y[0][:, 0:C], 1.0 / (L1_HEADS * L1_DIM), EPS, ALU.mult, ALU.add))
                dve.wait_ge(root, b + 1)
                chain(dve.reciprocal(r, rms[:, 1, :]))
                chain(dve.tensor_tensor(t1, r, r, ALU.mult))
                chain(dve.tensor_tensor(t1, t1, var, ALU.mult))
                chain(dve.tensor_scalar(t1, t1, -0.5, 1.5, ALU.mult, ALU.add))
                chain(dve.tensor_tensor(r, r, t1, ALU.mult))
                if b == BATCH - 1:
                    add_to_x(b)

            @block.tensor
            def _(pe):
                def fill(n, bank, ready, count_in):
                    if n < ROW_FILLS:
                        pe.wait_ge(w_in[n % RAW], count_in)
                        src = w_raw[:, n % RAW, :].rearrange("p (c n) -> p c n", n=P)
                    else:
                        pe.wait_ge(o_in, count_in)
                        src = o_raw[:, :, chunk(n - ROW_FILLS)]
                    for c in range(KC):
                        mm = pe.transpose(bank[:, chunk(c)], src[:, c, :], ident_f[:, :])
                    mm.then_inc(ready, 1)

                def next_fill(it, n, bank, ready):
                    fill(n, bank, ready,
                         16 * (ROW_FILLS // RAW * (it + 1) + n // RAW + 1) if n < ROW_FILLS else 16 * (it + 2))

                def accumulate(out, pairs, sem):
                    for n, (lhs, rhs) in enumerate(pairs):
                        mm = pe.matmul(out, lhs, rhs, start=(n == 0), stop=(n == len(pairs) - 1))
                    if sem is not None:
                        mm.then_inc(sem, 1)
                    return mm

                n_tensor(pe)
                for n in range(FILLS if b == 0 else 0):
                    if n >= NP_:
                        pe.wait_ge(p_read[n % NP_], n // NP_)
                    fill(n, ps_p[n % NP_], p_ready, 16 * (n // RAW + 1) if n < ROW_FILLS else 16)
                pe.wait_ge(lo_done, SEQ_TILES)
                with pe.Fori(TURNS * b, TURNS * (b + 1)) as it:
                    for s in range(NP_):
                        pe.wait_ge(p_read[s], p_reads(it, s) - 1)
                    for event in ORDER:
                        kind = event[0]
                        if event in IN_P:
                            n = IN_P.index(event)
                            bank = ps_p[n % NP_]
                            if n >= NP_:
                                pe.wait_ge(p_read[n % NP_], p_reads(it, n) - 1)
                            if kind == "fill":
                                next_fill(it, event[1], bank, p_ready)
                            elif kind == "v":
                                t = event[1]
                                accumulate(bank[:, 0:HP * P],
                                           [(x[:, c, chunk(t)], w[:, c, :, :].rearrange("p h n -> p (h n)"))
                                            for x, w in passes((xT_hi, xT_lo), v_T) for c in range(KC)], p_ready)
                            else:
                                _, h, s = event
                                accumulate(bank[:, :],
                                           [(w[:, "qkg".index(kind), h, c, :], x[:, c, half(s)])
                                            for w, x in passes(w_T, (xT_hi, xT_lo)) for c in range(KC)], p_ready)
                            continue
                        if kind == "project":
                            t = event[1]
                            pe.wait_ge(y_read[t % NY], CREDIT + C // NY * it + t // NY)
                            if t % CH == 0:
                                pe.wait_ge(ylo_ready, CREDIT + HP * H * it + gated(HP - 1, t // CH) + 1)
                            accumulate(ps_y[t % NY][:, :],
                                       [(y[:, h, chunk(t)], w[:, h, :]) for h in range(HP)
                                        for y, w in passes((y_hi, y_lo), o_T)], y_ready)
                            continue
                        n = IN_A.index(event)
                        bank = ps_a[n % NA]
                        pe.wait_ge(a_read[n % NA], CREDIT + a_reads(it, n) - 1)
                        if kind == "fill":
                            next_fill(it, event[1], bank, a_ready)
                            continue
                        _, h, s = event
                        chunks = range(CH * s, CH * s + CH)
                        if kind == "turn_k":
                            wait_evacuated(pe, it, ("k", h, s))
                            for c in chunks:
                                mm = pe.transpose(bank[:, chunk(c % CH)], kT[:, h, chunk(c)], ident_f[:, :])
                        if kind == "score":
                            wait_evacuated(pe, it, ("q", h, s))
                            for c in chunks:
                                mm = pe.matmul(bank[:, chunk(c % CH)], kT[:, h, chunk(c)], qT[:, h, chunk(c)],
                                               start=True, stop=True)
                        if kind == "update":
                            wait_evacuated(pe, it, ("turn_k", h, s))
                            if s == 0:
                                wait_evacuated(pe, it, ("v", C - 2))
                                wait_evacuated(pe, it, ("v", C - 1))
                            for c in chunks:
                                if c < C - 1:
                                    mm = pe.matmul(bank[:, chunk(c % CH)], kd[:, chunk(c)], v[:, c, h * P:(h + 1) * P],
                                                   start=True, stop=True)
                        if kind == "out":
                            wait_evacuated(pe, it, ("score", h, s))
                            if s == 0:
                                pe.wait_ge(qd_ready, CREDIT + HP * it + h + 1)
                            for c in chunks:
                                pairs = [(v[:, c, h * P:(h + 1) * P], sc[:, chunk(c)])]
                                if c > 0:
                                    pe.wait_ge(state_ready, (C - 1) * (HP * it + h) + c)
                                    pairs.append((state[:, c, :], qd[:, chunk(c)]))
                                mm = accumulate(bank[:, chunk(c % CH)], pairs, None)
                        mm.then_inc(a_ready, 1)
                pe.wait_ge(cleared, 3 * b + 3)
                pe.wait_ge(sq_added, CREDIT + HP * H * DONE)
                for s in range(NY):
                    pe.wait_ge(y_read[s], CREDIT + C // NY * DONE)
                for t in range(C):
                    mm = pe.matmul(ps_y[0][:, t:t + 1], sq_sum[:, chunk(t)], ones[:, :], start=True, stop=True,
                                   skip_group_check=True)
                mm.then_inc(sum_ready, 1)


RANKS = (8, 16, 32, 64)


def routed_ffn(nc, banks, X, w_raw, a_raw, lb_raw, raw_in, b_dram, gate_b_dram, out_dram, stats_in, ident_f):
    with ExitStack() as ctx:
        core = Core(nc, ctx)
        MAX_R, NR = RANKS[-1], len(RANKS)
        COLS = DIM + MAX_R + NR
        HALF = COLS // 2
        REST = DIM - HALF
        w_hi = core.sb("ffn1_w_hi", [P, KC, COLS], F32R)
        w_lo = core.sb("ffn1_w_lo", [P, KC, COLS], F32R)
        lb_T = core.sb("ffn1_lb_T", [MAX_R, DIM])
        bias = core.sb("ffn1_bias", [P, DIM])
        gate_b = core.sb("ffn1_gate_b", [P, NR])
        mu = core.sb("ffn1_mu", [P, TILES])
        rstd = core.sb("ffn1_rstd", [P, TILES])
        xn = core.sb("ffn1_xn", [P, 2, DIM])
        xT_hi = core.sb("ffn1_xT_hi", [P, 2, DIM], F32R)
        xT_lo = core.sb("ffn1_xT_lo", [P, 2, DIM], F32R)
        logit = core.sb("ffn1_logit", [P, 2, NR])
        expd = core.sb("ffn1_exp", [P, 2, NR])
        neg_max = core.sb("ffn1_neg_max", [P, 2, 1])
        total = core.sb("ffn1_total", [P, 2, 1])
        prob = core.sb("ffn1_prob", [P, 2, NR])
        best = core.sb("ffn1_best", [P, 2, 1])
        weight = core.sb("ffn1_weight", [P, 2, 1])
        other = core.sb("ffn1_other", [P, 2, NR])
        keep = core.sb("ffn1_keep", [P, 2, NR])
        lora = core.sb("ffn1_lora", [P, 2, MAX_R])
        lora_T = core.sb("ffn1_lora_T", [MAX_R, 2, P])
        ps_xT, ps_a, ps_b, (ps_l, ps_lT) = banks[0:2], banks[2:4], banks[4:6], banks[6:8]

        bias_in = core.sem("ffn1_bias_in")
        turned = core.sem("ffn1_turned")
        w_hi_done = core.sem("ffn1_w_hi_done")
        w_done = core.sem("ffn1_w_done")
        lb_done = core.sem("ffn1_lb_done")
        normed = core.sem("ffn1_normed")
        transposed = core.sem("ffn1_transposed")
        hi_done = core.sem("ffn1_hi_done")
        lo_done = core.sem("ffn1_lo_done")
        projected = core.sem("ffn1_projected")
        route = core.sem("ffn1_route")
        exp_done = core.sem("ffn1_exp_done")
        masked = core.sem("ffn1_masked")
        lora_turned = core.sem("ffn1_lora_turned")
        lora_kept = core.sem("ffn1_lora_kept")
        lora_done = core.sem("ffn1_lora_done")
        added = core.sem("ffn1_added")
        biased = core.sem("ffn1_biased")
        finished = core.sem("ffn1_finished")
        stored = core.sem("ffn1_stored")
        ROUTE = 11

        ln_vector, ln_scalar = layernorm_scales(core, "ffn1", stats_in, mu, rstd, lambda dve: None)

        with nc.Block() as block:
            @block.sync
            def _(sp):
                sp.dma_start(bias[:, :], b_dram.unsqueeze(0).broadcast_to([P, DIM])).then_inc(bias_in, 16)
                sp.dma_start(gate_b[:, :], gate_b_dram.unsqueeze(0).broadcast_to([P, NR])).then_inc(bias_in, 16)
                out_v = out_dram.rearrange("b (t p) d -> p (b t) d", p=P)
                for t in range(0, TILES, 2):
                    sp.wait_ge(finished, t + 2)
                    sp.dma_start(out_v[:, t:t + 2, :], X[:, t:t + 2, :]).then_inc(stored, 16)
                sp.wait_ge(stored, 16 * TILES // 2)

            @block.gpsimd
            def _(pool):
                pool.wait_ge(bias_in, 32)
                for t in range(TILES):
                    pool.wait_ge(normed, t + 1)
                    nc.gpsimd.tensor_tensor(X[:, t, :], X[:, t, :], bias[:, :], ALU.add).then_inc(biased, 1)

            def w_columns(w, n):
                if n < KC:
                    return w[:, :, n * P:(n + 1) * P]
                return w[:, :, DIM:COLS]

            def w_bank(n):
                width = P if n < KC else MAX_R + NR
                return ps_xT[n % 2][:, 0:KC * width].rearrange("p (c n) -> p c n", n=width)

            @block.scalar
            def _(act):
                ln_scalar(act)
                for n in range(KC + 1):
                    act.wait_ge(turned, n + 1)
                    nc.scalar.copy(w_columns(w_hi, n), w_bank(n)).then_inc(w_hi_done, 1)
                act.wait_ge(turned, KC + 2)
                nc.scalar.copy(lb_T[:, :], ps_lT[0:MAX_R, :]).then_inc(lb_done, 1)
                for s in range(-1, TILES + 2):
                    t = s + 1
                    if t < TILES:
                        act.wait_ge(transposed, t + 1)
                        if t >= 2:
                            act.wait_ge(projected, t - 1)
                        nc.scalar.copy(xT_hi[:, t % 2, :], ps_xT[t % 2][:, :]).then_inc(hi_done, 1)
                    t = s - 1
                    if 0 <= t < TILES:
                        i = t % 2
                        act.wait_ge(route, ROUTE * t + 2)
                        nc.scalar.activation(expd[:, i, :], logit[:, i, :], ACT.Exp, bias=neg_max[:, i, :],
                                             accum_out=total[:, i, :]).then_inc(exp_done, 1)
                    t = s - 2
                    if t >= 0:
                        i = t % 2
                        act.wait_ge(lora_turned, t + 1)
                        if t >= 2:
                            act.wait_ge(lora_done, t - 1)
                        nc.scalar.copy(lora_T[:, i, :], ps_lT[0:MAX_R, 0:P]).then_inc(lora_kept, 1)

            @block.vector
            def _(dve):
                ln_vector(dve)
                for n in range(KC + 1):
                    dve.wait_ge(w_hi_done, n + 1)
                    dve.tensor_tensor(w_columns(w_lo, n), w_bank(n), w_columns(w_hi, n), ALU.subtract
                                      ).then_inc(w_done, 1)
                dve.wait_ge(bias_in, 32)
                step = [0]

                def link(ins):
                    step[0] += 1
                    ins.then_inc(route, 1)

                def linked():
                    dve.wait_ge(route, step[0])

                def chain(ins):
                    link(ins)
                    linked()

                def routing(t, between):
                    i = t % 2
                    a = MAX_R + REST
                    dve.wait_ge(projected, t + 1)
                    chain(dve.tensor_tensor(logit[:, i, :], ps_b[i][:, a:a + NR], gate_b[:, :], ALU.add))
                    chain(dve.tensor_reduce(neg_max[:, i, :], logit[:, i, :], AX_X, ALU.max, negate=True))
                    between[0]()
                    dve.wait_ge(exp_done, t + 1)
                    link(dve.reciprocal(total[:, i, :], total[:, i, :]))
                    between[1]()
                    linked()
                    chain(dve.tensor_scalar(prob[:, i, :], expd[:, i, :], total[:, i, :], None, ALU.mult))
                    link(dve.tensor_reduce(best[:, i, :], prob[:, i, :], AX_X, ALU.max))
                    between[2]()
                    linked()
                    link(dve.reciprocal(weight[:, i, :], best[:, i, :]))
                    link(dve.tensor_scalar(other[:, i, :], prob[:, i, :], best[:, i, :], None, ALU.not_equal))
                    linked()
                    link(dve.tensor_tensor(weight[:, i, :], weight[:, i, :], best[:, i, :], ALU.mult))
                    between[3]()
                    linked()
                    for n in range(NR - 1):
                        before = keep[:, i, n - 1:n] if n else weight[:, i, :]
                        chain(dve.tensor_tensor(keep[:, i, n:n + 1], before, other[:, i, n:n + 1], ALU.mult))
                    if t >= 2:
                        dve.wait_ge(lora_turned, t - 1)
                    for n in range(NR):
                        lo = 0 if n == 0 else RANKS[n - 1]
                        by = weight[:, i, :] if n == 0 else keep[:, i, n - 1:n]
                        dve.tensor_scalar(lora[:, i, lo:RANKS[n]], ps_b[i][:, REST + lo:REST + RANKS[n]], by, None,
                                          ALU.mult).then_inc(masked, 1)

                def normalize(t):
                    if t < TILES:
                        if t >= 2:
                            dve.wait_ge(transposed, t - 1)
                        dve.tensor_scalar(xn[:, t % 2, :], X[:, t, :], mu[:, t:t + 1], rstd[:, t:t + 1],
                                          ALU.subtract, ALU.mult).then_inc(normed, 1)

                def add_products(t):
                    i = t % 2
                    dve.wait_ge(biased, t + 1)
                    dve.tensor_tensor(X[:, t, 0:HALF], X[:, t, 0:HALF], ps_a[i][:, 0:HALF], ALU.add
                                      ).then_inc(added, 1)
                    dve.tensor_tensor(X[:, t, HALF:DIM], X[:, t, HALF:DIM], ps_b[i][:, 0:REST], ALU.add
                                      ).then_inc(added, 1)

                def finish(t):
                    if t >= 0:
                        dve.wait_ge(lora_done, t + 1)
                        dve.wait_ge(added, 2 * t + 2)
                        dve.tensor_tensor(X[:, t, :], X[:, t, :], ps_l[:, :], ALU.add).then_inc(finished, 1)

                normalize(0)
                normalize(1)
                for s in range(-1, TILES + 1):
                    t = s + 1
                    if t < TILES:
                        dve.wait_ge(hi_done, t + 1)
                        if t >= 2:
                            dve.wait_ge(projected, t - 1)
                        dve.tensor_tensor(xT_lo[:, t % 2, :], ps_xT[t % 2][:, :], xT_hi[:, t % 2, :],
                                          ALU.subtract).then_inc(lo_done, 1)
                    t = s - 1
                    if t >= 0:
                        routing(t, [lambda: finish(s - 3), lambda: add_products(t), lambda: None,
                                    lambda: normalize(s + 2)])
                    elif s >= 0:
                        normalize(s + 2)
                for t in range(TILES - 2, TILES):
                    finish(t)

            @block.tensor
            def _(pe):
                pe.wait_ge(raw_in, 64)
                for n in range(KC + 1):
                    if n >= 2:
                        pe.wait_ge(w_done, n - 1)
                    bank = w_bank(n)
                    for c in range(KC):
                        if n < KC:
                            mm = pe.transpose(bank[:, c, :], w_raw[:, n, c * P:(c + 1) * P], ident_f[:, :])
                        else:
                            rows = MAX_R + NR
                            mm = pe.transpose(bank[:, c, :], a_raw[:, c * P:(c + 1) * P], ident_f[0:rows, 0:rows])
                    mm.then_inc(turned, 1)
                for c in range(KC):
                    mm = pe.transpose(ps_lT[0:MAX_R, c * P:(c + 1) * P], lb_raw[:, c, :], ident_f[:, :])
                mm.then_inc(turned, 1)

                def transpose_x(t):
                    pe.wait_ge(normed, t + 1)
                    if t >= 2:
                        pe.wait_ge(lo_done, t - 1)
                    else:
                        pe.wait_ge(w_done, KC + 1)
                    for c in range(KC):
                        mm = pe.transpose(ps_xT[t % 2][:, c * P:(c + 1) * P], xn[:, t % 2, c * P:(c + 1) * P],
                                          ident_f[:, :])
                    mm.then_inc(transposed, 1)

                transpose_x(0)
                transpose_x(1)
                pe.wait_ge(lb_done, 1)

                def turn_lora(t):
                    if t >= 0:
                        pe.wait_ge(masked, NR * (t + 1))
                        if t >= 1:
                            pe.wait_ge(lora_kept, t)
                        pe.transpose(ps_lT[0:MAX_R, 0:P], lora[:, t % 2, :], ident_f[:, :]).then_inc(lora_turned, 1)

                for s in range(TILES + 2):
                    t = s
                    if t < TILES:
                        pe.wait_ge(lo_done, t + 1)
                        if t >= 2:
                            pe.wait_ge(masked, NR * (t - 1))
                            pe.wait_ge(added, 2 * (t - 1))
                        for ps, a in ((ps_a[t % 2], 0), (ps_b[t % 2], HALF)):
                            if a:
                                turn_lora(t - 2)
                            n = 0
                            for x, w in passes((xT_hi, xT_lo), (w_hi, w_lo)):
                                for c in range(KC):
                                    mm = pe.matmul(ps[:, 0:HALF], x[:, t % 2, c * P:(c + 1) * P], w[:, c, a:a + HALF],
                                                   start=(n == 0), stop=(n == 3 * KC - 1))
                                    n += 1
                        mm.then_inc(projected, 1)
                        if t + 2 < TILES:
                            transpose_x(t + 2)
                    else:
                        turn_lora(t - 2)
                    t = s - 2
                    if t >= 0:
                        pe.wait_ge(lora_kept, t + 1)
                        if t >= 1:
                            pe.wait_ge(finished, t)
                        pe.matmul(ps_l[:, :], lora_T[:, t % 2, :], lb_T[:, :], start=True, stop=True
                                  ).then_inc(lora_done, 1)


def l1_constants():
    import numpy as np

    f = np.float32
    base = f(1.0 / 2.0 ** (8.0 / L1_HEADS))
    factor = f(1.0 - 1 / (32 - 1 + 1e-05) + 1e-05)
    slope = ((base ** (np.arange(L1_HEADS, dtype=f) + f(1.0))) * factor).astype(np.float64)
    r = np.arange(P, dtype=np.float64)
    distance = r[None, :] - r[:, None]
    decay = np.where(distance >= 0, np.exp(-slope[:, None, None] * np.maximum(distance, 0)), 0.0)
    q_decay = np.exp(-slope[:, None] * (r + 1))
    k_decay = np.exp(-slope[:, None] * (P - 1 - r))
    scales = np.stack([k_decay.T, np.broadcast_to(np.exp(-slope * P), (P, L1_HEADS))], -1)
    pairs = L1_HEADS // 2
    return {
        "decay": decay.astype(f).reshape(pairs, 2, P, P),
        "qdec": q_decay.astype(f).reshape(pairs, 2, P),
        "scales": np.ascontiguousarray(scales.astype(f).reshape(P, pairs, 2, 2).transpose(1, 0, 2, 3)),
    }


def preln_layers(nc, ins, out):
    QT_dram = nc.dram_tensor("stacked_q", (BATCH * HEADS, STACK, SEQ), BF16, kind="Internal").ap()
    KT_dram = nc.dram_tensor("stacked_k", (BATCH * KV_HEADS, STACK, SEQ), BF16, kind="Internal").ap()
    with ExitStack() as ctx:
        core = Core(nc, ctx)
        banks = core.banks()
        X = core.sb("X", [P, TILES, DIM])
        ident_f = core.sb("identity_f32", [P, P])
        ident_b = core.sb("identity_bf16", [P, P], BF16)
        mask_s = core.sb("mask_query_key", [P, P], BF16)
        mask_t = core.sb("mask_key_query", [P, P], BF16)
        stats = [core.sb(f"stats{n}", [P, TILES, 6]) for n in range(2)]
        masks = core.sb("masks_f32", [P, 2, P])
        constants_in = core.sem("constants_in")
        constants_cast = core.sem("constants_cast")
        with nc.Block() as block:
            @block.sync
            def _(sp):
                for to, name in ((ident_f[:, :], "ident_f"), (masks[:, 0, :], "mask_s"), (masks[:, 1, :], "mask_t")):
                    sp.dma_start(to, ins[name]).then_inc(constants_in, 16)

            @block.vector
            def _(dve):
                dve.wait_ge(constants_in, 48)
                for to, src in ((ident_b, ident_f[:, :]), (mask_s, masks[:, 0, :]), (mask_t, masks[:, 1, :])):
                    dve.tensor_copy(to[:, :], src).then_inc(constants_cast, 1)
                dve.wait_ge(constants_cast, 3)
        with ExitStack() as layer0:
            part = Core(nc, layer0)
            V = part.sb("V_parts", [P, BATCH * KV_HEADS, SEQ_TILES, V_COLS], BF16)
            stackT = part.sb("qk_stackT", [STACK, 2, HEADS + KV_HEADS, 2, P], BF16)
            stored = part.sems("stack_stored", 2)
            project_qkv(nc, banks, ins["L0_attn_x"], ins["L0_attn_Wq"], ins["L0_attn_Wk"], ins["L0_attn_Wv"],
                        ins["rope_cos"], ins["rope_sin"], X, V, ident_f, ident_b, QT_dram, KT_dram, stackT, stored)
            wo = [part.sb(f"wo_{name}", [P, KC, DIM], F32R) for name in ("hi", "lo")]
            w_ffn0 = [part.sb(f"ffn0_{name}", [P, KC, DIM], F32R) for name in ("hi", "lo")]
            O = part.sb("attention_out", [P, BATCH * KC, SEQ_TILES, P])
            prefetch = [(ins["L0_attn_Wo"], *wo), (ins["L0_ffn_kernel"], *w_ffn0)]
            softmax_attend(nc, banks, stored, prefetch, V, O, QT_dram, KT_dram, ident_f, ident_b, mask_s, mask_t)
            project_tiles(nc, banks, "wo", X, *wo, ident_f, stats[0],
                          source=lambda t: O[:, KC * (t // SEQ_TILES):KC * (t // SEQ_TILES + 1), t % SEQ_TILES, :])
            project_tiles(nc, banks, "ffn0", X, *w_ffn0, ident_f, stats[1], stats_in=stats[0],
                          bias=ins["L0_ffn_bias"])
        kT = core.sb("l1_kT", [P, L1_PAIR, SEQ])
        qd = core.sb("l1_qd", [P, SEQ])
        w_raw = kT[:, :, :].rearrange("p h (o d) -> p (h o) d", d=DIM)
        a_raw = qd[0:RANKS[-1] + len(RANKS), 0:DIM]
        lb_raw = qd[:, DIM:DIM + KC * RANKS[-1]].rearrange("p (o r) -> p o r", r=RANKS[-1])
        ffn1_raw_in = core.sem("ffn1_raw_in")
        ffn1_loads = [(w_raw, ins["L1_ffn_W"].rearrange("(o p) d -> p o d", p=P)),
                      (a_raw[0:RANKS[-1], :], ins["L1_ffn_A"]), (a_raw[RANKS[-1]:, :], ins["L1_ffn_gate_w"]),
                      (lb_raw, ins["L1_ffn_B"].rearrange("(o p) r -> p o r", p=P))]
        with ExitStack() as layer1:
            part = Core(nc, layer1)
            xT_hi = part.sb("l1_xT_hi", [P, KC, SEQ], F32R)
            xT_lo = part.sb("l1_xT_lo", [P, KC, SEQ], F32R)
            buffers = linear_attend_buffers(part, kT, qd)
            sems = linear_attend_semaphores(part)
            mu, rstd = (part.sb(f"l1_{name}", [P, TILES]) for name in ("mu", "rstd"))
            for b in range(BATCH):
                linear_attend(nc, banks, buffers, sems, b, X, mu, rstd, xT_hi, xT_lo, ins["L1_attn_qkv_w"],
                              ins["L1_attn_out_w"], ins["L1_attn_gate_w"], ins["L1_attn_norm_w"], ins["decay"],
                              ins["qdec"], ins["scales"], stats[1], stats[0], ident_f,
                              (ffn1_loads, ffn1_raw_in) if b == BATCH - 1 else None)
        routed_ffn(nc, banks, X, w_raw, a_raw, lb_raw, ffn1_raw_in, ins["L1_ffn_b"], ins["L1_ffn_gate_b"], out, stats[0], ident_f)


def shape_constants():
    import numpy as np

    f = np.float32
    inv = (f(1) / (f(10000) ** (np.arange(0, HEAD_DIM, 2, dtype=f) / f(HEAD_DIM)))).astype(f)
    angle = np.arange(SEQ, dtype=f)[:, None] * inv[None, :]
    cos = np.repeat(np.cos(angle), 2, axis=1)
    sin = np.repeat(np.sin(angle), 2, axis=1) * np.tile([-1, 1], HEAD_DIM // 2)

    def by_tile(a):
        return np.ascontiguousarray(a.reshape(SEQ_TILES, P, HEAD_DIM).transpose(1, 0, 2).astype(f))

    i = np.arange(P)
    mask = np.where(i[None, :] <= i[:, None], 0, -1e30).astype(f)
    return {"ident_f": np.eye(P, dtype=f), "mask_s": mask,
            "mask_t": np.ascontiguousarray(mask.T), "rope_cos": by_tile(cos), "rope_sin": by_tile(sin),
            **l1_constants()}


def kernel(**inputs):
    import concourse.bacc as bacc
    import numpy as np
    from concourse.bass_utils import run_bass_kernel_spmd

    nc = bacc.Bacc("TRN2", target_bir_lowering=False, num_devices=1)
    arrays, aps = {}, {}
    for name, a in {**inputs, **shape_constants()}.items():
        a = np.ascontiguousarray(a)
        arrays[f"in_{name}"] = a
        aps[name] = nc.dram_tensor(f"in_{name}", a.shape, mybir.dt.from_np(a.dtype), kind="ExternalInput").ap()
    out = nc.dram_tensor("out_0", (BATCH, SEQ, DIM), F32, kind="ExternalOutput").ap()
    preln_layers(nc, aps, out)
    result = run_bass_kernel_spmd(nc, [arrays], core_ids=[0])
    return result.results[0]["out_0"]
```
